# Optimizing a Trainium2 kernel written in Bass

```python
import numpy as np
import jax
import jax.numpy as jnp

def _softmax(x, axis=-1):
    return jax.nn.softmax(x, axis=axis)

def _gelu(x):
    return jax.nn.gelu(x, approximate=True)

def _silu(x):
    return jax.nn.silu(x)

def _sigmoid(x):
    return jax.nn.sigmoid(x)

def _layernorm(x, axis=-1, eps=1e-05):
    m = jnp.mean(x, axis=axis, keepdims=True)
    v = jnp.var(x, axis=axis, keepdims=True)
    return (x - m) / jnp.sqrt(v + eps)

def _scatter_add(tgt, idx, src, axis=0):
    return tgt.at[idx].add(src)

def _segment_sum(src, seg, n):
    return jax.ops.segment_sum(src, seg, n)
kernel_name = 'mk_early_fusion_d1_tok_img256_r4_fdeaf4'

def setup_inputs(seed: int=0):
    np.random.seed(seed)
    _w = jnp.asarray

    def _rec_inputs():
        import jax
        import jax.numpy as jnp
        _rk = jax.random.key(seed)
        x = -7.10856e-05 + 0.999911 * jax.random.normal(jax.random.fold_in(_rk, 1), (8, 64, 128, 64), jnp.float32)
        txt = -0.000161634 + 0.479995 * jax.random.normal(jax.random.fold_in(_rk, 2), (8, 32, 64), jnp.float32)
        return (x, txt)
    x, txt = _rec_inputs()

    def _L0_tok_setup():
        import jax, jax.numpy as jnp
        import numpy as np
        PATCH_LEN = 16
        STRIDE = 8
        PAD = 8
        key = jax.random.key(seed)
        k1, k2 = jax.random.split(key)
        x = jax.random.normal(k1, (32, 64, 128, 64), dtype=jnp.float32)
        in_feat = 64 * (PATCH_LEN // 2 + 1) * 2
        W = jax.random.normal(k2, (64, in_feat), dtype=jnp.float32) * 0.02
        return {'x': x, 'W': W}
    _L0_tok_all = _L0_tok_setup()
    _L0_tok_in = {k: v for k, v in _L0_tok_all.items() if k in ('W',)}
    del _L0_tok_all

    def _L0_attn_setup():
        import jax, jax.numpy as jnp
        import numpy as np
        DIM = 64
        NUM_HEADS = 4
        HEAD_DIM = DIM // NUM_HEADS
        SCALE = HEAD_DIM ** (-0.5)
        key = jax.random.key(seed)
        k1, k2, k3, k4 = jax.random.split(key, 4)
        B, N, C = (2, 1024, DIM)
        x = jax.random.normal(k1, (B, N, C), dtype=jnp.float32)
        w_qkv = jax.random.normal(k2, (3 * C, C), dtype=jnp.float32) * C ** (-0.5)
        w_proj = jax.random.normal(k3, (C, C), dtype=jnp.float32) * C ** (-0.5)
        b_proj = jax.random.normal(k4, (C,), dtype=jnp.float32) * 0.02
        return {'x': x, 'w_qkv': w_qkv, 'w_proj': w_proj, 'b_proj': b_proj}
    _L0_attn_all = _L0_attn_setup()
    _L0_attn_in = {k: v for k, v in _L0_attn_all.items() if k in ('w_qkv', 'w_proj', 'b_proj')}
    del _L0_attn_all

    def _L0_ffn_setup():
        import jax, jax.numpy as jnp
        import numpy as np
        B, T, D, H, E = (16, 1024, 64, 128, 8)
        key = jax.random.key(seed)
        ks = jax.random.split(key, 5)
        x = jax.random.normal(ks[0], (B, T, D), dtype=jnp.float32)
        gate_w = jax.random.normal(ks[1], (D, E), dtype=jnp.float32) * 0.02
        gate_b = jnp.zeros((E,), dtype=jnp.float32)
        W1 = jax.random.normal(ks[2], (E, D, H), dtype=jnp.float32) * 0.02
        b1 = jnp.zeros((E, H), dtype=jnp.float32)
        W2 = jax.random.normal(ks[3], (E, H, D), dtype=jnp.float32) * 0.02
        b2 = jnp.zeros((E, D), dtype=jnp.float32)
        return {'x': x, 'gate_w': gate_w, 'gate_b': gate_b, 'W1': W1, 'b1': b1, 'W2': W2, 'b2': b2}
    _L0_ffn_all = _L0_ffn_setup()
    _L0_ffn_in = {k: v for k, v in _L0_ffn_all.items() if k in ('gate_w', 'gate_b', 'W1', 'b1', 'W2', 'b2')}
    del _L0_ffn_all
    return {'x': x, 'txt': txt, 'L0_tok_W': _L0_tok_in['W'], 'L0_attn_w_qkv': _L0_attn_in['w_qkv'], 'L0_attn_w_proj': _L0_attn_in['w_proj'], 'L0_attn_b_proj': _L0_attn_in['b_proj'], 'L0_ffn_gate_w': _L0_ffn_in['gate_w'], 'L0_ffn_gate_b': _L0_ffn_in['gate_b'], 'L0_ffn_W1': _L0_ffn_in['W1'], 'L0_ffn_b1': _L0_ffn_in['b1'], 'L0_ffn_W2': _L0_ffn_in['W2'], 'L0_ffn_b2': _L0_ffn_in['b2']}

def reference(x, txt, L0_tok_W, L0_attn_w_qkv, L0_attn_w_proj, L0_attn_b_proj, L0_ffn_gate_w, L0_ffn_gate_b, L0_ffn_W1, L0_ffn_b1, L0_ffn_W2, L0_ffn_b2):
    import jax
    import jax.numpy as jnp

    def _L0_tok_ref(x, W):
        import jax, jax.numpy as jnp
        import numpy as np
        PATCH_LEN = 16
        STRIDE = 8
        PAD = 8
        B, C, T, V = x.shape
        xp = jnp.pad(x, ((0, 0), (0, 0), (0, PAD), (0, 0)), mode='edge')
        Tp = T + PAD
        N = (Tp - PATCH_LEN) // STRIDE + 1
        idx = jnp.arange(N)[:, None] * STRIDE + jnp.arange(PATCH_LEN)[None, :]
        patches = xp[:, :, idx, :]
        patches = jnp.transpose(patches, (0, 4, 2, 3, 1))
        xf = jnp.fft.rfft(patches, axis=-2, norm='ortho')
        F = xf.shape[-2]
        x_real = xf.real.reshape(B, V, N, F * C)
        x_imag = xf.imag.reshape(B, V, N, F * C)
        x_emb = jnp.concatenate([x_real, x_imag], axis=-1)
        x_emb = x_emb @ W.T
        return x_emb.reshape(B, V * N, -1)

    def _L0_attn_ref(x, w_qkv, w_proj, b_proj):
        import jax, jax.numpy as jnp
        import numpy as np
        DIM = 64
        NUM_HEADS = 4
        HEAD_DIM = DIM // NUM_HEADS
        SCALE = HEAD_DIM ** (-0.5)
        B, N, C = x.shape
        H, D = (NUM_HEADS, HEAD_DIM)
        qkv = x @ w_qkv.T
        qkv = qkv.reshape(B, N, 3, H, D).transpose(2, 0, 3, 1, 4)
        q, k, v = (qkv[0], qkv[1], qkv[2])
        attn = jnp.einsum('bhnd,bhmd->bhnm', q, k) * SCALE
        attn = jax.nn.softmax(attn, axis=-1)
        out = jnp.einsum('bhnm,bhmd->bhnd', attn, v)
        out = out.transpose(0, 2, 1, 3).reshape(B, N, C)
        out = out @ w_proj.T + b_proj
        return out

    def _L0_ffn_ref(x, gate_w, gate_b, W1, b1, W2, b2):
        import jax, jax.numpy as jnp
        import numpy as np
        B, T, D, H, E = (16, 1024, 64, 128, 8)
        Bb, Tt, Dd = x.shape
        Ee = gate_w.shape[1]
        xf = x.reshape(-1, Dd)
        N = xf.shape[0]
        logits = xf @ gate_w + gate_b
        probs = jax.nn.softmax(logits, axis=-1)
        top2_vals, top2_idx = jax.lax.top_k(probs, 2)
        cw = jnp.zeros((N, Ee), dtype=xf.dtype).at[jnp.arange(N)[:, None], top2_idx].add(top2_vals)

        def step(acc, params):
            w1, bb1, w2, bb2, we = params
            h = jax.nn.gelu(xf @ w1 + bb1, approximate=False)
            y = h @ w2 + bb2
            return (acc + we[:, None] * y, None)
        out, _ = jax.lax.scan(step, jnp.zeros_like(xf), (W1, b1, W2, b2, cw.T))
        return out.reshape(Bb, Tt, Dd)
    h = _L0_tok_ref(x, L0_tok_W)
    h = jnp.concatenate([h, txt], axis=1)
    h = h + _L0_attn_ref(_layernorm(h, axis=-1), L0_attn_w_qkv, L0_attn_w_proj, L0_attn_b_proj)
    h = h + _L0_ffn_ref(_layernorm(h, axis=-1), L0_ffn_gate_w, L0_ffn_gate_b, L0_ffn_W1, L0_ffn_b1, L0_ffn_W2, L0_ffn_b2)
    return h

_drawn_inputs = setup_inputs


def setup_inputs(seed=0):
    import zlib

    import numpy as np

    out = dict(_drawn_inputs(seed))
    spreads = {'L0_ffn_gate_b': (0.0, 0.1), 'L0_ffn_b1': (0.0, 0.8), 'L0_ffn_b2': (0.0, 0.1)}
    factors = {'L0_ffn_W1': 7.059, 'L0_ffn_W2': 6.027}
    for name, (base, spread) in spreads.items():
        noise = np.random.default_rng([zlib.crc32(name.encode()), seed]).standard_normal(out[name].shape)
        drawn = base * np.exp(spread * noise) if base else spread * noise
        out[name] = jnp.asarray(drawn.astype(out[name].dtype))
    for name, factor in factors.items():
        out[name] = (out[name] * factor).astype(out[name].dtype)
    return out
```

```python
from contextlib import ExitStack

import concourse.bass as bass
from concourse import mybir

F32 = mybir.dt.float32
BF16 = mybir.dt.bfloat16
ALU = mybir.AluOpType
ACT = mybir.ActivationFunctionType
AX = mybir.AxisListType

P = 128
B, C, T, V = 8, 64, 128, 64
TXT = 32
D = 64
PATCH, STRIDE = 16, 8
NPATCH = T // STRIDE
NFREQ = PATCH // 2 + 1
IMG = V * NPATCH
L = IMG + TXT
H, DH = 4, 16
E, HID = 8, 128
PAIRS = B // 2
CH = L // 3
NCH = 3
KT = IMG // P
HALF = IMG // 2
SCALE = float(DH) ** -0.5
EPS = 1e-5
ROWS = 6 * DH
UNITS = NCH * (1 + KT * H)
GROUPS = NCH * KT
QT = H * KT
MAXU = 2 * QT + 2 + NCH
PARTS = [(0, 0), (0, 1), (1, 0), (0, 2), (1, 1), (2, 0)]

C_ID, C_CENTRE, C_MEAN, C_DEN, C_FOLD, C_DFT, C_ORDER = 0, 128, 256, 384, 512, 576, 592
C_COLS = 600

AT_PROJECT = [0, 2, 4, 6, 8]
AT_FINISH = [12, 16, 20, 24, 28, 32]
AT_TOKENISE = [36, 42, 48, 52, 54, 56, 60, 62, 64]
FIRST_MAX = 20
AT_SHIFT = FIRST_MAX + 69
PV_LAG = 2 * H

N_SETUP = 11
SHIFT_DMAS = 3 * (H + 1)
N_FFN = 8
PRESETS = 18

USES = {"tokenise": (5, 4), "project": (3, 2), "shift": (1, 0), "finish": (3, 3)}


def side_banks(stage):
    n = [0, 0]
    out = []
    for i in range(sum(USES[stage])):
        out.append((i % 2, n[i % 2]))
        n[i % 2] += 1
    return out


def plus(g, stage):
    return (g[0] + USES[stage][0], g[1] + USES[stage][1])


def build(nc, x, txt, tok_w, w_qkv, w_proj, b_proj, gate_w, gate_b, w1, b1, w2, b2, consts, out):
    with ExitStack() as ctx:
        def sb(name, shape, dt=F32):
            return ctx.enter_context(nc.sbuf_tensor(name, shape, dt))

        def bank(name):
            return ctx.enter_context(nc.psum_tensor(name, [P, 512], F32))

        def sem(name):
            return ctx.enter_context(nc.semaphore(name))

        cw_dram = nc.dram_tensor("gates_by_expert", [E, B * L], F32, kind="Internal").ap()

        cst = sb("cst", [P, C_COLS])
        ident = cst[:, C_ID:C_ID + P]
        centre = cst[:, C_CENTRE:C_CENTRE + P]
        mean = cst[:, C_MEAN:C_MEAN + P]
        den_sel = cst[:, C_DEN:C_DEN + P]
        fold = cst[:, C_FOLD:C_FOLD + D]
        qkv_in = sb("qkv_in", [P, 2, D])
        v_in = sb("v_in", [D, 2, D])
        proj_in = sb("proj_in", [D, H, 32])
        qkT = sb("qkT", [P, P])
        vT = sb("vT", [P, D])
        projT = sb("projT", [P, D])
        proj_bias = sb("proj_bias", [P, 1])
        gate_sb = sb("gate_sb", [P, E])
        gate_bias = sb("gate_bias", [P, E])
        w1_sb = sb("w1_sb", [P, E, HID])
        w2_sb = sb("w2_sb", [P, E, D])
        biases = sb("biases", [P, E + E // 2])
        b1_sb, b2_sb = biases[:, 0:E], biases[:, E:E + E // 2]
        bias_in = sb("bias_in", [E + E // 2, P])
        tok_m = sb("tok_m", [P, 8, D])
        h2_all = sb("h2_all", [P, PAIRS, L])

        banks = [bank(f"bank{i}") for i in range(8)]
        score_bank = banks[0:3]
        o_bank = banks[3]
        max_bank = banks[4:6]
        side_bank = banks[6:8]

        setup_loaded = sem("setup_loaded")
        ffn_loaded = sem("ffn_loaded")
        preset = sem("preset")
        setup_psum = sem("setup_psum")
        setup_done = sem("setup_done")
        x_loaded = sem("x_loaded")
        side_full = [sem("side_full0"), sem("side_full1")]
        side_free = [sem("side_free0"), sem("side_free1")]
        rstd_act = sem("rstd_act")
        rstd_dve = sem("rstd_dve")
        xn_ready = sem("xn_ready")
        h_copied = sem("h_copied")
        h_stored = sem("h_stored")
        part1_done = sem("part1_done")
        part2_done = sem("part2_done")
        part3_done = sem("part3_done")
        stacked = sem("stacked")
        v_ready = sem("v_ready")
        max_scores = sem("max_scores")
        max_done = sem("max_done")
        neg_max = sem("neg_max")
        shift_step = sem("shift_step")
        shifted = sem("shifted")
        scores_ready = sem("scores_ready")
        exp_done = sem("exp_done")
        pv_done = sem("pv_done")
        o_ready = sem("o_ready")
        o_free = sem("o_free")
        recip_done = sem("recip_done")
        on_ready = sem("on_ready")

        phase1 = ExitStack()

        def sb1(name, shape, dt=F32):
            return phase1.enter_context(nc.sbuf_tensor(name, shape, dt))

        xt = [sb1(f"x{i}", [P, NPATCH + 1, 4, V]) for i in range(2)]
        text_in = sb1("text_in", [TXT, 2, D])
        h_new = sb1("h_new", [P, L])
        h_res = sb1("h_res", [P, L])
        xc = sb1("xc", [P, L])
        sq = sb1("sq", [P, L])
        var = sb1("var", [P, L])
        rstd = sb1("rstd", [P, L])
        rstd_sq = sb1("rstd_sq", [P, L])
        xn = sb1("xn", [P, L])
        qk_part = [sb1(f"qk_part{i}", [P, L], BF16) for i in range(3)]
        qk_rest = sb1("qk_rest", [P, L])
        qs = [sb1(f"q_stack{i}", [P, H, L], BF16) for i in range(2)]
        ks = [sb1(f"k_stack{i}", [P, H, L], BF16) for i in range(2)]
        v_tiles = [sb1(f"v_tiles{i}", [P, KT, H, 32]) for i in range(2)]
        v_tail = [sb1(f"v_tail{i}", [P, P]) for i in range(2)]
        max_parts = sb1("max_parts", [P, QT, 3])
        max_tail = sb1("max_tail", [P, NCH])
        negm = sb1("negm", [P, P])
        m_part = sb1("m_part", [QT + 1, 3, P], BF16)
        m_rest = sb1("m_rest", [QT + 1, P])
        probs = sb1("probs", [P, 3, H, CH])
        tok_in = probs[0:2 * NFREQ, :, :, :].rearrange("r i h l -> r (i h l)")[:, 0:D * C]\
            .rearrange("r (d c) -> r d c", c=C)
        probs_tail = [sb1(f"probs_tail{i}", [P, CH]) for i in range(NCH)]
        ot = [sb1(f"heads_out{i}", [P, L]) for i in range(2)]
        recip = sb1("recip", [P, L])
        on = sb1("on", [P, L])

        g_tok0 = (0, 0)
        g_prj0 = plus(g_tok0, "tokenise")
        g_shf0 = plus(g_prj0, "project")
        g_slot0 = plus(g_shf0, "shift")
        g_slot1 = plus(plus(plus(g_slot0, "project"), "tokenise"), "shift")
        g_slot2 = plus(plus(plus(g_slot1, "project"), "finish"), "shift")
        per_round = tuple(USES["tokenise"][i] + 2 * (USES["project"][i] + USES["finish"][i] + USES["shift"][i])
                          for i in range(2))

        def slot_plan(odd, q):
            g = tuple((g_slot1 if odd else g_slot2)[i] + per_round[i] * q for i in range(2))
            b = 2 * q + (1 if odd else 2)
            return b, g

        def side_steps(u, stages, b, q, g):
            order = []
            if "project" in stages:
                if u in AT_PROJECT:
                    order.append(("project", AT_PROJECT.index(u), g))
                g = plus(g, "project")
            if "finish" in stages:
                if u in AT_FINISH:
                    order.append(("finish", AT_FINISH.index(u), g))
                g = plus(g, "finish")
            if "tokenise" in stages:
                if u in AT_TOKENISE:
                    order.append(("tokenise", AT_TOKENISE.index(u), g))
                g = plus(g, "tokenise")
            if "maxima" in stages:
                if FIRST_MAX <= u < FIRST_MAX + MAXU:
                    order.append(("maxima", u - FIRST_MAX, g))
                if u == AT_SHIFT:
                    order.append(("shift", 0, g))
            if "load" in stages and u == 0:
                order.append(("load", 0, g))
            return order

        BESIDE = {0: ("project", "tokenise", "maxima"), "odd": ("load", "project", "finish", "maxima"),
                  "even": ("project", "finish", "tokenise", "maxima"), 5: ("project", "finish", "maxima"),
                  6: ("project", "finish", "maxima"), 7: ("finish",)}

        def run_phase1(eng, attend_unit, side, after_slot):
            def slot(b, par, q, g, stages):
                for u in range(UNITS):
                    attend_unit(b, par, u, g)
                    for stage, i, gg in side_steps(u, stages, b, q, g):
                        side(stage, i, b, par, q, gg)
                after_slot(b, par)

            for i in range(sum(USES["tokenise"])):
                side("tokenise", i, -2, 0, -2, g_tok0)
            for i in range(sum(USES["project"])):
                side("project", i, -1, 1, -1, g_prj0)
            for u in range(MAXU):
                side("maxima", u, -1, 1, -1, g_shf0)
            side("shift", 0, -1, 1, -1, g_shf0)
            slot(0, 0, -1, g_slot0, BESIDE[0])
            with eng.Fori(0, 2) as q:
                b, g = slot_plan(True, q)
                slot(b, 1, q, g, BESIDE["odd"])
                b, g = slot_plan(False, q)
                slot(b, 0, q, g, BESIDE["even"])
            b, g = slot_plan(True, 2)
            slot(b, 1, 2, g, BESIDE[5])
            b, g = slot_plan(False, 2)
            slot(b, 0, 2, g, BESIDE[6])
            g7 = plus(plus(plus(g, "project"), "finish"), "shift")
            slot(7, 1, 3, g7, BESIDE[7])
            g8 = plus(g7, "finish")
            for i in range(sum(USES["finish"])):
                side("finish", i, 8, 0, 3, g8)

        def at_least(eng, s, value):
            if not isinstance(value, int) or value > 0:
                eng.wait_ge(s, value)

        def full(eng, stage, i, g):
            k, n = side_banks(stage)[i]
            eng.wait_ge(side_full[k], g[k] + n + 1)
            return side_bank[k]

        def bank_of(stage, i):
            return side_banks(stage)[i][0]

        def freed(eng, stage, i, g):
            k, n = side_banks(stage)[i]
            eng.wait_ge(side_free[k], g[k] + n + 1)

        def free_bank(eng, stage, i, g):
            k, n = side_banks(stage)[i]
            at_least(eng, side_free[k], g[k] + n)
            return side_bank[k]

        X_DMAS = 9
        chunk = [slice(c * CH, (c + 1) * CH) for c in range(NCH)]

        def guess_rstd(act, var, rstd, rstd_sq, c, n, done):
            nc.scalar.activation(rstd_sq[:, chunk[c]], var[:, chunk[c]], ACT.Ln).then_inc(done, 1)
            act.wait_ge(done, 3 * n + 1)
            nc.scalar.activation(rstd[:, chunk[c]], rstd_sq[:, chunk[c]], ACT.Exp, scale=-0.5).then_inc(done, 1)
            act.wait_ge(done, 3 * n + 2)
            nc.scalar.activation(rstd_sq[:, chunk[c]], rstd[:, chunk[c]], ACT.Square).then_inc(done, 1)

        def refine_rstd(dve, var, rstd, rstd_sq, c, n, guessed, done):
            dve.wait_ge(guessed, 3 * n + 3)
            nc.vector.scalar_tensor_tensor(out=rstd_sq[:, chunk[c]], in0=var[:, chunk[c]], scalar=-0.5,
                                           in1=rstd_sq[:, chunk[c]], op0=ALU.mult, op1=ALU.mult).then_inc(done, 1)
            dve.wait_ge(done, 2 * n + 1)
            nc.vector.scalar_tensor_tensor(out=rstd[:, chunk[c]], in0=rstd_sq[:, chunk[c]], scalar=1.5,
                                           in1=rstd[:, chunk[c]], op0=ALU.add, op1=ALU.mult).then_inc(done, 1)

        with nc.Block() as block:

            @block.sync
            def _(sp):
                def load_x(pair):
                    for bp in range(2):
                        src = x[bass.ds(2 * pair + bp, 1)].rearrange("o c t v -> (o c) t v")
                        for th in range(2):
                            part = slice(C * th, C * th + C)
                            sp.dma_start(xt[bp][part, 0:NPATCH, :, :],
                                         src.rearrange("c (j h t) v -> h c j t v", h=2, t=4)[th])\
                              .then_inc(x_loaded, 16)
                            sp.dma_start(xt[bp][part, NPATCH, :, :],
                                         src[:, T - 1:T, :].broadcast_to([C, 4, V])).then_inc(x_loaded, 16)
                    sp.dma_start(text_in[:, :, :], txt[bass.ds(2 * pair, 2)].rearrange("b t d -> t b d"))\
                      .then_inc(x_loaded, 16)

                sp.dma_start(cst[:, :], consts).then_inc(setup_loaded, 16)
                sp.dma_start(tok_in[:, :, :], tok_w.rearrange("d (r c) -> r d c", c=C)).then_inc(setup_loaded, 16)
                for s in range(2):
                    for half in range(2):
                        sp.dma_start(qkv_in[D * s:D * s + D, half, :],
                                     w_qkv[D * s:D * s + D, :].rearrange("(h d) c -> d h c", h=H))\
                          .then_inc(setup_loaded, 16)
                for half in range(2):
                    sp.dma_start(v_in[:, half, :], w_qkv[2 * D:3 * D, :]).then_inc(setup_loaded, 16)
                sp.dma_start(bias_in[0:E, :], b1).then_inc(setup_loaded, 16)
                sp.dma_start(bias_in[E:E + E // 2, :], b2.rearrange("(k o) n -> k (o n)", o=2))\
                  .then_inc(setup_loaded, 16)
                sp.wait_ge(preset, 1)
                sp.dma_start(proj_in[:, :, 0:DH], w_proj.rearrange("n (h d) -> n h d", h=H)).then_inc(setup_loaded, 16)
                load_x(0)
                for half in range(2):
                    rows = slice(D * half, D * half + D)
                    sp.dma_start(proj_bias[rows, :], b_proj.rearrange("(n o) -> n o", o=1)).then_inc(ffn_loaded, 16)
                    sp.dma_start(gate_sb[rows, :], gate_w).then_inc(ffn_loaded, 16)
                    sp.dma_start(w1_sb[rows, :, :], w1.rearrange("e c n -> c e n")).then_inc(ffn_loaded, 16)
                sp.dma_start(gate_bias[:, :], gate_b.rearrange("(o e) -> o e", o=1).broadcast_to([P, E]))\
                  .then_inc(ffn_loaded, 16)
                sp.dma_start(w2_sb[:, :, :], w2.rearrange("e n c -> n e c")).then_inc(ffn_loaded, 16)

                def attend_unit(b, par, u, g):
                    pass

                def side(stage, i, b, par, q, g):
                    nxt = 1 - par
                    if stage == "project" and i == 4:
                        sp.wait_ge(part1_done, NCH * (b + 2))
                        sp.wait_ge(part2_done, NCH * (b + 2))
                        sp.wait_ge(part3_done, NCH * (b + 2))
                        for t, (a, k) in enumerate(PARTS):
                            rows = slice(DH * t, DH * t + DH)
                            sp.dma_start(qs[nxt][rows, :, :], qk_part[a][0:D, :]).then_inc(stacked, 16)
                            sp.dma_start(ks[nxt][rows, :, :], qk_part[k][D:P, :]).then_inc(stacked, 16)
                    elif stage == "shift":
                        sp.wait_ge(shift_step, 3 * (b + 2))
                        for t in range(3):
                            row = slice(ROWS + t, ROWS + t + 1)
                            for h in range(H):
                                sp.dma_start(qs[nxt][row, h, 0:IMG], m_part[KT * h:KT * h + KT, t, :]).then_inc(shifted, 16)
                            sp.dma_start(qs[nxt][row, :, IMG:L], m_part[QT:QT + 1, t, :]).then_inc(shifted, 16)
                    elif stage == "load":
                        sp.wait_ge(xn_ready, NCH * (q + 2))
                        load_x(q + 2)
                    elif stage == "tokenise" and i == 2 and isinstance(b, int) and b < 0:
                        sp.wait_ge(side_full[0], 2)
                        sp.wait_ge(side_full[1], 1)
                        load_x(1)
                    elif stage == "tokenise" and i == 0 and isinstance(b, int) and b == 0:
                        sp.wait_ge(xn_ready, NCH)
                        sp.dma_start(h_res[:, :], h_new[:, :]).then_inc(h_copied, 16)
                    elif stage == "finish" and i == 5 and par == 0:
                        freed(sp, "finish", 5, g)
                        sp.dma_start(h2_all[:, bass.ds(q, 1), :].rearrange("p o l -> p (o l)"), h_res[:, :])\
                          .then_inc(h_stored, 16)
                        sp.wait_ge(h_stored, 16 * (q + 1))
                        if not (isinstance(b, int) and b == B):
                            sp.wait_ge(xn_ready, NCH * (q + 2))
                            sp.dma_start(h_res[:, :], h_new[:, :]).then_inc(h_copied, 16)

                run_phase1(nc.sync, attend_unit, side, lambda b, par: None)
                sp.wait_ge(ffn_loaded, 16 * N_FFN)

            @block.gpsimd
            def _(pool):
                def side(stage, i, b, par, q, g):
                    if stage == "tokenise" and i >= 6:
                        c = i - 6
                        pool.wait_ge(rstd_dve, 2 * (NCH * (q + 2) + c + 1))
                        nc.gpsimd.tensor_tensor(xn[:, chunk[c]], xc[:, chunk[c]], rstd[:, chunk[c]], ALU.mult)\
                          .then_inc(xn_ready, 1)
                    elif stage == "project" and i < 3:
                        pool.wait_ge(part2_done, NCH * (b + 1) + i + 1)
                        at_least(pool, stacked, 16 * 12 * (b + 1))
                        nc.gpsimd.tensor_tensor(qk_part[2][:, chunk[i]], qk_rest[:, chunk[i]], qk_part[1][:, chunk[i]],
                                                ALU.subtract).then_inc(part3_done, 1)
                    elif stage == "finish" and i % 2 == 0:
                        freed(pool, "finish", i, g)
                        c = i // 2
                        nc.gpsimd.tensor_tensor(on[:, chunk[c]], ot[1 - par][:, chunk[c]], recip[:, chunk[c]], ALU.mult)\
                          .then_inc(on_ready, 1)

                run_phase1(nc.gpsimd, lambda b, par, u, g: None, side, lambda b, par: None)

            @block.scalar
            def _(act):
                act.wait_ge(setup_psum, 1)
                nc.scalar.activation(qkT[:, :], banks[0][:, 0:P], ACT.Copy)
                nc.scalar.activation(vT[:, :], banks[0][:, P:P + D], ACT.Copy)
                nc.scalar.activation(biases[:, :], banks[0][:, 2 * P:2 * P + E + E // 2], ACT.Copy)
                nc.scalar.activation(projT[:, :], banks[0][:, P + D:P + 2 * D], ACT.Copy).then_inc(setup_done, 1)

                def evacuate_o(b, par, qc):
                    act.wait_ge(o_ready, NCH * b + qc + 1)
                    nc.scalar.activation(ot[par][:, chunk[qc]], o_bank[:, 0:CH], ACT.Copy).then_inc(o_free, 1)

                def attend_unit(b, par, u, g):
                    qc, r = divmod(u, 1 + KT * H)
                    act.wait_ge(scores_ready, UNITS * b + u + 1)
                    src = score_bank[u % 3][:, 0:CH]
                    if r == 0:
                        nc.scalar.activation(probs_tail[qc][:, :], src, ACT.Exp, scale=SCALE).then_inc(exp_done, 1)
                        return
                    kt, h = divmod(r - 1, H)
                    group = KT * qc + kt
                    if h == 0:
                        at_least(act, pv_done, GROUPS * b + group - 2)
                    nc.scalar.activation(probs[:, group % 3, h, :], src, ACT.Exp, scale=SCALE).then_inc(exp_done, 1)
                    if r == 6 and qc > 0:
                        evacuate_o(b, par, qc - 1)

                def side(stage, i, b, par, q, g):
                    nxt = 1 - par
                    if stage == "project":
                        bank = full(act, "project", i, g)
                        if i < 3:
                            at_least(act, stacked, 16 * 12 * (b + 1))
                            nc.scalar.activation(qk_part[0][:, chunk[i]], bank[:, 0:CH], ACT.Copy).then_inc(part1_done, 1)
                        elif i == 3:
                            nc.scalar.activation(v_tiles[nxt][:, :, :, 0:DH].rearrange("p k h d -> p (k h) d"),
                                                 bank[:, :].rearrange("p (k d) -> p k d", d=DH), ACT.Copy)\
                              .then_inc(side_free[bank_of("project", i)], 1)
                        else:
                            for h in range(H):
                                rows = slice(32 * h, 32 * h + 32)
                                last = nc.scalar.activation(v_tail[nxt][rows, 32 * h:32 * h + DH], bank[rows, 0:DH], ACT.Copy)
                            last.then_inc(side_free[bank_of("project", i)], 1)
                    elif stage == "tokenise" and i in (0, 2):
                        bank = full(act, "tokenise", i, g)
                        at_least(act, h_copied, 16 * (q + 2))
                        cols, n = (slice(0, HALF), HALF) if i == 0 else (slice(IMG, L), TXT)
                        nc.scalar.activation(h_new[:, cols], bank[:, 0:n], ACT.Copy)\
                          .then_inc(side_free[bank_of("tokenise", i)], 1)
                    elif stage == "tokenise" and 3 <= i < 6:
                        c = i - 3
                        bank = full(act, "tokenise", i, g)
                        nc.scalar.activation(xc[:, chunk[c]], bank[:, 0:CH], ACT.Copy)
                        nc.scalar.activation(sq[:, chunk[c]], bank[:, 0:CH], ACT.Square)\
                          .then_inc(side_free[bank_of("tokenise", i)], 1)
                    elif stage == "tokenise" and i >= 6:
                        freed(act, "tokenise", i, g)
                        guess_rstd(act, var, rstd, rstd_sq, i - 6, NCH * (q + 2) + i - 6, rstd_act)

                run_phase1(nc.scalar, attend_unit, side, lambda b, par: evacuate_o(b, par, NCH - 1))

            @block.vector
            def _(dve):
                nc.vector.memset(proj_in[:, :, :], 0.0).then_inc(preset, 1)
                for i in range(2):
                    nc.vector.memset(v_tiles[i][:, :, :, :], 0.0).then_inc(preset, 1)
                    nc.vector.memset(v_tail[i][:, :], 0.0).then_inc(preset, 1)
                    nc.vector.memset(ks[i][ROWS:ROWS + 3, :, :], 1.0).then_inc(preset, 1)
                nc.vector.memset(negm[:, :], 0.0).then_inc(preset, 1)
                dve.wait_ge(preset, 8)
                for i in range(2):
                    nc.vector.memset(v_tiles[i][:, :, :, DH:DH + 1], 1.0).then_inc(preset, 1)
                    for h in range(H):
                        nc.vector.memset(v_tail[i][32 * h:32 * h + 32, 32 * h + DH:32 * h + DH + 1], 1.0)\
                          .then_inc(preset, 1)
                dve.wait_ge(setup_psum, 2)
                nc.vector.tensor_copy(tok_m[:, :, :].rearrange("p k d -> p d k"),
                                      banks[1][:, :].rearrange("p (d k) -> p d k", k=8)).then_inc(setup_done, 1)

                def side(stage, i, b, par, q, g):
                    nxt = 1 - par
                    if stage == "maxima":
                        n = MAXU * (b + 1) + i
                        dve.wait_ge(max_scores, n + 1)
                        src = max_bank[(nxt + i) % 2]
                        if i < 2 * QT:
                            nc.vector.tensor_reduce(max_parts[:, i // 2, i % 2:i % 2 + 1], src[:, :], AX.X, ALU.max)\
                              .then_inc(max_done, 1)
                        elif i < 2 * QT + 2:
                            part = slice(16 * (i - 2 * QT), 16 * (i - 2 * QT) + 16)
                            nc.vector.tensor_reduce(max_parts[:, part, 2],
                                                    src[:, :].rearrange("p (n k) -> p n k", k=TXT), AX.X, ALU.max)\
                              .then_inc(max_done, 1)
                        else:
                            c = i - 2 * QT - 2
                            nc.vector.tensor_reduce(max_tail[:, c:c + 1], src[:, 0:CH], AX.X, ALU.max)\
                              .then_inc(max_done, 1)
                        if i == MAXU - 1:
                            dve.wait_ge(max_done, MAXU * (b + 2))
                            nc.vector.tensor_reduce(negm[:, 0:QT], max_parts[:, :, :], AX.X, ALU.max, negate=True)\
                              .then_inc(neg_max, 1)
                            nc.vector.tensor_reduce(negm[:, QT:QT + 1], max_tail[:, :], AX.X, ALU.max, negate=True)\
                              .then_inc(neg_max, 1)
                    elif stage == "shift":
                        bank = full(dve, "shift", 0, g)
                        at_least(dve, shifted, 16 * SHIFT_DMAS * (b + 1))
                        src = bank[0:QT + 1, 0:P]
                        nc.vector.tensor_copy(m_part[:, 0, :], src).then_inc(shift_step, 1)
                        dve.wait_ge(shift_step, 3 * (b + 1) + 1)
                        nc.vector.tensor_tensor(m_rest[:, :], src, m_part[:, 0, :], ALU.subtract)\
                          .then_inc(side_free[bank_of("shift", 0)], 1)
                        freed(dve, "shift", 0, g)
                        nc.vector.tensor_copy(m_part[:, 1, :], m_rest[:, :]).then_inc(shift_step, 1)
                        dve.wait_ge(shift_step, 3 * (b + 1) + 2)
                        nc.vector.tensor_tensor(m_part[:, 2, :], m_rest[:, :], m_part[:, 1, :], ALU.subtract)\
                          .then_inc(shift_step, 1)
                    elif stage == "project" and i < 3:
                        k = bank_of("project", i)
                        dve.wait_ge(part1_done, NCH * (b + 1) + i + 1)
                        at_least(dve, part3_done, NCH * (b + 1))
                        at_least(dve, stacked, 16 * 12 * (b + 1))
                        nc.vector.tensor_tensor(qk_rest[:, chunk[i]], side_bank[k][:, 0:CH], qk_part[0][:, chunk[i]],
                                                ALU.subtract).then_inc(side_free[k], 1)
                        freed(dve, "project", i, g)
                        nc.vector.tensor_copy(qk_part[1][:, chunk[i]], qk_rest[:, chunk[i]]).then_inc(part2_done, 1)
                    elif stage == "tokenise" and i == 1:
                        bank = full(dve, "tokenise", i, g)
                        at_least(dve, h_copied, 16 * (q + 2))
                        nc.vector.tensor_copy(h_new[:, HALF:IMG], bank[:, :]).then_inc(side_free[bank_of("tokenise", i)], 1)
                    elif stage == "tokenise" and i >= 6:
                        c = i - 6
                        bank = full(dve, "tokenise", i, g)
                        nc.vector.tensor_scalar(var[:, chunk[c]], bank[:, 0:CH], EPS, None, ALU.add)\
                          .then_inc(side_free[bank_of("tokenise", i)], 1)
                        refine_rstd(dve, var, rstd, rstd_sq, c, NCH * (q + 2) + c, rstd_act, rstd_dve)
                    elif stage == "finish":
                        bank = full(dve, "finish", i, g)
                        c = i // 2
                        if i % 2 == 0:
                            nc.vector.reciprocal(recip[:, chunk[c]], bank[:, 0:CH])\
                              .then_inc(side_free[bank_of("finish", i)], 1)
                        else:
                            rows = slice(D * nxt, D * nxt + D)
                            dve.wait_ge(h_copied, 16 * (q + 1))
                            dve.wait_ge(ffn_loaded, 16 * N_FFN)
                            nc.vector.scalar_tensor_tensor(out=h_res[rows, chunk[c]], in0=bank[rows, 0:CH],
                                                           scalar=proj_bias[rows, :], in1=h_res[rows, chunk[c]],
                                                           op0=ALU.add, op1=ALU.add)\
                              .then_inc(side_free[bank_of("finish", i)], 1)

                run_phase1(nc.vector, lambda b, par, u, g: None, side, lambda b, par: None)

            @block.tensor
            def _(pe):
                pe.wait_ge(setup_loaded, 16 * N_SETUP)
                nc.tensor.transpose(banks[0][:, 0:P], qkv_in[:, :, :].rearrange("p a c -> p (a c)"), ident)
                nc.tensor.transpose(banks[0][:, P:P + D], v_in[:, :, :].rearrange("p a c -> p (a c)"), ident[0:D, 0:D])
                nc.tensor.transpose(banks[0][:, P + D:P + 2 * D], proj_in[:, :, :].rearrange("p h d -> p (h d)"),
                                    ident[0:D, 0:D])
                nc.tensor.transpose(banks[0][:, 2 * P:2 * P + E + E // 2], bias_in[:, :],
                                    ident[0:E + E // 2, 0:E + E // 2]).then_inc(setup_psum, 1)
                for d in range(D):
                    for th in range(2):
                        last = nc.tensor.matmul(banks[1][C * th:C * th + C, 8 * d:8 * d + 8], tok_in[:, d, :],
                                                cst[0:2 * NFREQ, C_DFT + 8 * th:C_DFT + 8 * th + 8],
                                                start=True, stop=True)
                last.then_inc(setup_psum, 1)
                pe.wait_ge(setup_done, 2)
                pe.wait_ge(preset, PRESETS)

                def heads_times_v(b, par, group, g):
                    qc, kt = divmod(group, KT)
                    pe.wait_ge(exp_done, UNITS * b + (1 + KT * H) * qc + 1 + H * kt + H)
                    if kt == 0:
                        at_least(pe, o_free, NCH * b + qc)
                        if qc == 0:
                            pe.wait_ge(side_free[0], g[0])
                            pe.wait_ge(side_free[1], g[1])
                    for h in range(H):
                        last = nc.tensor.matmul(o_bank[32 * h:32 * h + 32, 0:CH], v_tiles[par][:, kt, h, :],
                                                probs[:, group % 3, h, :], start=(kt == 0), stop=False,
                                                skip_group_check=True)
                    last.then_inc(pv_done, 1)
                    if kt == KT - 1:
                        nc.tensor.matmul(o_bank[:, 0:CH], v_tail[par][:, :], probs_tail[qc][:, :], start=False, stop=True,
                                         skip_group_check=True).then_inc(o_ready, 1)

                def attend_unit(b, par, u, g):
                    qc, r = divmod(u, 1 + KT * H)
                    if u == 0:
                        pe.wait_ge(shifted, 16 * SHIFT_DMAS * (b + 1))
                    at_least(pe, exp_done, UNITS * b + u - 2)
                    bank = score_bank[u % 3]
                    if r == 0:
                        for h in range(H):
                            last = nc.tensor.matmul(bank[32 * h:32 * h + 32, 0:CH], ks[par][0:ROWS + 3, h, IMG:L],
                                                    qs[par][0:ROWS + 3, h, chunk[qc]], start=True, stop=True)
                    else:
                        kt, h = divmod(r - 1, H)
                        last = nc.tensor.matmul(bank[:, 0:CH], ks[par][0:ROWS + 3, h, P * kt:P * kt + P],
                                                qs[par][0:ROWS + 3, h, chunk[qc]], start=True, stop=True)
                    last.then_inc(scores_ready, 1)
                    chunk_of, step = divmod(u - PV_LAG, 1 + KT * H)
                    if chunk_of >= 0 and step % H == 0 and step < H * KT:
                        heads_times_v(b, par, KT * chunk_of + step // H, g)

                def side(stage, i, b, par, q, g):
                    nxt = 1 - par
                    rows = slice(D * nxt, D * nxt + D)
                    if stage == "maxima":
                        n = MAXU * (b + 1) + i
                        if i == 0:
                            pe.wait_ge(stacked, 16 * 12 * (b + 2))
                        at_least(pe, max_done, n - 1)
                        bank = max_bank[(nxt + i) % 2]
                        if i < 2 * QT:
                            h, t = divmod(i // 2, KT)
                            last = nc.tensor.matmul(bank[:, :], qs[nxt][0:ROWS, h, P * t:P * t + P],
                                                    ks[nxt][0:ROWS, h, HALF * (i % 2):HALF * (i % 2) + HALF],
                                                    start=True, stop=True)
                        elif i < 2 * QT + 2:
                            for j in range(16):
                                h, t = divmod(16 * (i - 2 * QT) + j, KT)
                                last = nc.tensor.matmul(bank[:, TXT * j:TXT * j + TXT], qs[nxt][0:ROWS, h, P * t:P * t + P],
                                                        ks[nxt][0:ROWS, h, IMG:L], start=True, stop=True)
                        else:
                            c = i - 2 * QT - 2
                            for h in range(H):
                                last = nc.tensor.matmul(bank[32 * h:32 * h + 32, 0:CH], qs[nxt][0:ROWS, h, IMG:L],
                                                        ks[nxt][0:ROWS, h, chunk[c]], start=True, stop=True)
                        last.then_inc(max_scores, 1)
                        return
                    if stage == "load":
                        return
                    if (stage, i) == ("project", 4):
                        bank = side_bank[bank_of(stage, i)]
                    else:
                        bank = free_bank(pe, stage, i, g)
                    if stage == "shift":
                        pe.wait_ge(neg_max, 2 * (b + 2))
                        last = nc.tensor.transpose(bank[:, 0:P], negm[:, :], ident)
                    elif stage == "project":
                        if i == 0:
                            pe.wait_ge(xn_ready, NCH * (q + 2))
                        if i < 3:
                            last = nc.tensor.matmul(bank[:, 0:CH], qkT[rows, :], xn[rows, chunk[i]], start=True, stop=True)
                        elif i == 3:
                            free_bank(pe, stage, 4, g)
                            for t in range(KT):
                                last = nc.tensor.matmul(bank[:, D * t:D * t + D], xn[rows, P * t:P * t + P], vT[rows, :],
                                                        start=True, stop=True)
                        else:
                            for h in range(H):
                                last = nc.tensor.matmul(bank[32 * h:32 * h + 32, 0:DH], xn[rows, IMG:L],
                                                        vT[rows, DH * h:DH * h + DH], start=True, stop=True)
                    elif stage == "tokenise":
                        if i == 0:
                            pe.wait_ge(x_loaded, 16 * X_DMAS * (q + 3))
                        if i < 2:
                            for k in range(8):
                                nxt_block, t4 = divmod(k, 4)
                                first = NPATCH // 2 * i + nxt_block
                                for bp in range(2):
                                    last = nc.tensor.matmul(bank[D * bp:D * bp + D, :], tok_m[:, k, :],
                                                            xt[bp][:, first:first + NPATCH // 2, t4, :],
                                                            start=(k == 0), stop=(k == 7), skip_group_check=True)
                        elif i == 2:
                            last = nc.tensor.matmul(bank[:, 0:TXT], text_in[:, :, :].rearrange("t b d -> t (b d)"),
                                                    ident[0:TXT, 0:TXT], start=True, stop=True)
                        elif i < 6:
                            if i == 3:
                                freed(pe, "tokenise", 1, g)
                                freed(pe, "tokenise", 2, g)
                            last = nc.tensor.matmul(bank[:, 0:CH], centre, h_new[:, chunk[i - 3]], start=True, stop=True)
                        else:
                            freed(pe, "tokenise", i - 3, g)
                            last = nc.tensor.matmul(bank[:, 0:CH], mean, sq[:, chunk[i - 6]], start=True, stop=True)
                    elif stage == "finish":
                        c = i // 2
                        if i == 0:
                            pe.wait_ge(o_free, NCH * b)
                        if i % 2 == 0:
                            last = nc.tensor.matmul(bank[:, 0:CH], den_sel, ot[nxt][:, chunk[c]], start=True, stop=True)
                        else:
                            pe.wait_ge(on_ready, NCH * (b - 1) + c + 1)
                            last = nc.tensor.matmul(bank[rows, 0:CH], projT[:, :], on[:, chunk[c]], start=True, stop=True)
                    last.then_inc(side_full[bank_of(stage, i)], 1)

                run_phase1(nc.tensor, attend_unit, side, lambda b, par: heads_times_v(b, par, GROUPS - 1, None))

        phase1.close()

        y2 = sb("x2_now", [P, L])
        x2_all = sb("x2_all", [P, PAIRS, L])
        xc2, sq2, var2 = sb("xc2", [P, L]), sb("sq2", [P, L]), sb("var2", [P, L])
        rstd2, rstd2_sq = sb("rstd2", [P, L]), sb("rstd2_sq", [P, L])
        S72 = B * (KT + 1)
        logits = sb("logits", [P, S72, E])
        gate_e = sb("gate_e", [P, S72, E])
        rest = sb("rest", [P, S72, E])
        hit = sb("hit", [P, S72, E])
        first_hot = sb("first_hot", [P, S72, E])
        top = sb("top", [P, S72, 1])
        total = sb("total", [P, S72, 1])
        cw_t = sb("cw_t", [D, B, P])
        cw_tail = sb("cw_tail", [D, TXT])
        x2 = [sb(f"x2_{i}", [P, L]) for i in range(2)]
        h2 = [sb(f"h2_{i}", [P, L]) for i in range(2)]
        cwb = [sb(f"cwb{i}", [P, E // 2, 2, L]) for i in range(2)]
        hid = sb("hid", [P, 4, CH])
        prod = sb("prod", [P, 4, CH])
        acc = sb("acc", [P, 2, L])
        outs = [[sb(f"outs{i}{j}", [P, KT, D]) for j in range(2)] for i in range(2)]
        out_tail = [[sb(f"out_tail{i}{j}", [TXT, D]) for j in range(2)] for i in range(2)]

        centred = sem("centred")
        sq_done = sem("sq_done")
        var_full = sem("var_full")
        var_read = sem("var_read")
        rstd2_act = sem("rstd2_act")
        rstd2_dve = sem("rstd2_dve")
        x2_ready = sem("x2_ready")
        x2_stored = sem("x2_stored")
        gate_full = sem("gate_full")
        gate_read = sem("gate_read")
        gate_step = sem("gate_step")
        gate_exp = sem("gate_exp")
        cw_full = sem("cw_full")
        cw_copied = sem("cw_copied")
        cw_stored = sem("cw_stored")
        loaded = [sem("loaded0"), sem("loaded1")]
        hid_full = sem("hid_full")
        gelu_done = sem("gelu_done")
        y_full = sem("y_full")
        y_read = sem("y_read")
        out_stored = sem("out_stored")
        zeroed = sem("zeroed")

        UPP = 2 * NCH
        KPP = UPP * E
        YPP = KPP // 2
        N_LOAD = 4
        ADDED = NCH * PAIRS
        order = cst[:, C_ORDER:C_ORDER + E]

        def over_slots(ap):
            return ap.unsqueeze(1).broadcast_to([P, S72, E])

        def over_experts(ap):
            return ap.broadcast_to([P, S72, E])

        with nc.Block() as block:
            @block.sync
            def _(sp):
                def norm_pair(p):
                    sp.wait_ge(x2_ready, NCH * p + NCH)
                    sp.dma_start(x2_all[:, bass.ds(p, 1), :].rearrange("p o l -> p (o l)"), y2[:, :])\
                      .then_inc(x2_stored, 16)

                norm_pair(0)
                with nc.sync.Fori(1, PAIRS) as p:
                    norm_pair(p)
                sp.wait_ge(cw_copied, 3)
                for b in range(B):
                    sp.dma_start(cw_dram[:, L * b:L * b + IMG].rearrange("e (t j) -> t e j", t=KT), cw_t[:, b, :])\
                      .then_inc(cw_stored, 16)
                sp.dma_start(cw_dram.rearrange("e (b l) -> b e l", b=B)[:, :, IMG:L], cw_tail[:, :])\
                  .then_inc(cw_stored, 16)
                sp.wait_ge(cw_stored, 16 * (B + 1))
                sp.wait_ge(x2_stored, 16 * PAIRS)

                def load(n):
                    s = n % 2
                    sp.dma_start(x2[s][:, :], x2_all[:, n, :]).then_inc(loaded[s], 16)
                    sp.dma_start(h2[s][:, :], h2_all[:, n, :]).then_inc(loaded[s], 16)
                    for o in range(2):
                        src = cw_dram.rearrange("(k o) (n l) -> o n k l", o=2, n=PAIRS)[o, n]
                        sp.dma_start(cwb[s][D * o:D * o + D, :, :, :].rearrange("p k b l -> p k (b l)"),
                                     src.unsqueeze(0).broadcast_to([D, E // 2, 2 * L])).then_inc(loaded[s], 16)

                def store(n):
                    for bp in range(2):
                        b = 2 * n + bp
                        sp.wait_ge(gate_read, B + b + 1)
                        rows = out[b, 0:IMG, :].rearrange("(v t o) c -> o v t c", t=KT, o=2)
                        for o in range(2):
                            sp.dma_start(rows[o], outs[n % 2][bp][V * o:V * o + V, :, :]).then_inc(out_stored, 16)
                        sp.dma_start(out[b, IMG:L, :], out_tail[n % 2][bp][:, :]).then_inc(out_stored, 16)

                load(0)
                load(1)
                for n in range(PAIRS):
                    store(n)
                    sp.wait_ge(out_stored, 16 * 6 * (n + 1))
                    if n + 2 < PAIRS:
                        load(n + 2)

            @block.gpsimd
            def _(pool):
                def norm_pair(p):
                    for c in range(NCH):
                        pool.wait_ge(rstd2_dve, 2 * (NCH * p + c + 1))
                        if c == 0:
                            at_least(pool, x2_stored, 16 * p)
                            at_least(pool, gate_full, 2 * p)
                        nc.gpsimd.tensor_tensor(y2[:, chunk[c]], xc2[:, chunk[c]], rstd2[:, chunk[c]], ALU.mult)\
                          .then_inc(x2_ready, 1)

                norm_pair(0)
                with nc.gpsimd.Fori(1, PAIRS) as p:
                    norm_pair(p)
                def pair(n, s, r):
                    pool.wait_ge(loaded[s], 16 * N_LOAD * (r + 1))
                    for v in range(UPP):
                        bp, c = divmod(v, NCH)
                        dst = acc[:, bp, chunk[c]]
                        first = YPP * n + 4 * v
                        done = 4 * (UPP * n + v)
                        if v % NCH == 0:
                            pool.wait_ge(gate_full, B + 2 * n)
                        pool.wait_ge(x2_ready, ADDED + done)
                        pool.wait_ge(y_read, first + 2)
                        nc.gpsimd.tensor_tensor(dst, prod[:, 0, :], prod[:, 1, :], ALU.add).then_inc(x2_ready, 1)
                        for k in (2, 3):
                            pool.wait_ge(y_read, first + k + 1)
                            pool.wait_ge(x2_ready, ADDED + done + k - 1)
                            nc.gpsimd.tensor_tensor(dst, dst, prod[:, k, :], ALU.add).then_inc(x2_ready, 1)
                        pool.wait_ge(x2_ready, ADDED + done + 3)
                        rows = slice(D * bp, D * bp + D)
                        nc.gpsimd.tensor_tensor(acc[rows, bp, chunk[c]], acc[rows, bp, chunk[c]],
                                                h2[s][rows, chunk[c]], ALU.add).then_inc(x2_ready, 1)

                with nc.gpsimd.Fori(0, PAIRS // 2) as r:
                    for s in range(2):
                        pair(2 * r + s, s, r)

            @block.scalar
            def _(act):
                def norm_pair(p):
                    at_least(act, x2_ready, NCH * p)
                    for c in range(NCH):
                        act.wait_ge(centred, NCH * p + c + 1)
                        nc.scalar.activation(xc2[:, chunk[c]], banks[c][:, 0:CH], ACT.Copy)
                        nc.scalar.activation(sq2[:, chunk[c]], banks[c][:, 0:CH], ACT.Square).then_inc(sq_done, 1)
                    for c in range(NCH):
                        act.wait_ge(var_read, NCH * p + c + 1)
                        guess_rstd(act, var2, rstd2, rstd2_sq, c, NCH * p + c, rstd2_act)

                norm_pair(0)
                with nc.scalar.Fori(1, PAIRS) as p:
                    norm_pair(p)
                act.wait_ge(gate_step, 2)
                nc.scalar.activation(gate_e[:, :, :], gate_e[:, :, :], ACT.Exp).then_inc(gate_exp, 1)

                with nc.scalar.Fori(0, PAIRS // 2) as r:
                    for s in range(2):
                        n = 2 * r + s
                        for v in range(UPP):
                            for e in range(E):
                                act.wait_ge(hid_full, KPP * n + E * v + e + 1)
                                if s > 0 or E * v + e >= 4:
                                    act.wait_ge(y_full, YPP * n + (E * v + e) // 2 - 1)
                                else:
                                    act.wait_ge(gate_full, B + 2 * n)
                                nc.scalar.activation(hid[:, e % 4, :], banks[e % 4][:, 0:CH], ACT.Gelu,
                                                     bias=b1_sb[:, e:e + 1]).then_inc(gelu_done, 1)
                            if v % NCH == NCH - 1:
                                bp = v // NCH
                                act.wait_ge(gate_full, B + 2 * n + bp + 1)
                                nc.scalar.activation(outs[s][bp][:, :, :].rearrange("p t c -> p (t c)"), banks[6][:, :],
                                                     ACT.Copy)
                                nc.scalar.activation(out_tail[s][bp][:, :], banks[7][0:TXT, 0:D], ACT.Copy)\
                                  .then_inc(gate_read, 1)

            @block.vector
            def _(dve):
                nc.vector.memset(logits[:, :, :], 0.0).then_inc(zeroed, 1)
                dve.wait_ge(zeroed, 1)
                def norm_pair(p):
                    for c in range(NCH):
                        dve.wait_ge(var_full, NCH * p + c + 1)
                        nc.vector.tensor_scalar(var2[:, chunk[c]], banks[3 + c][:, 0:CH], EPS, None, ALU.add)\
                          .then_inc(var_read, 1)
                    for c in range(NCH):
                        refine_rstd(dve, var2, rstd2, rstd2_sq, c, NCH * p + c, rstd2_act, rstd2_dve)
                    for bp in range(2):
                        dve.wait_ge(gate_full, 2 * p + bp + 1)
                        nc.vector.tensor_tensor(
                            logits[:, bass.ds(KT * (2 * p + bp), KT), :],
                            banks[6 + bp][:, 0:KT * E].rearrange("p (t e) -> p t e", e=E),
                            gate_bias[:, :].unsqueeze(1).broadcast_to([P, KT, E]), ALU.add)
                        nc.vector.tensor_tensor(
                            logits[0:TXT, bass.ds(KT * B + 2 * p + bp, 1), :].rearrange("p o e -> p (o e)"),
                            banks[6 + bp][0:TXT, KT * E:KT * E + E], gate_bias[0:TXT, :], ALU.add)\
                          .then_inc(gate_read, 1)

                norm_pair(0)
                with nc.vector.Fori(1, PAIRS) as p:
                    norm_pair(p)
                dve.wait_ge(gate_read, B)

                lg = logits[:, :, :]
                steps = [0]

                def step(ins):
                    ins.then_inc(gate_step, 1)
                    steps[0] += 1
                    dve.wait_ge(gate_step, steps[0])

                v = nc.vector
                step(v.tensor_reduce(top[:, :, :], lg, AX.X, ALU.max))
                step(v.tensor_tensor(gate_e[:, :, :], lg, over_experts(top[:, :, :]), ALU.subtract))
                step(v.tensor_tensor(hit[:, :, :], lg, over_experts(top[:, :, :]), ALU.is_equal))
                step(v.tensor_tensor(hit[:, :, :], hit[:, :, :], over_slots(order), ALU.mult))
                step(v.tensor_reduce(top[:, :, :], hit[:, :, :], AX.X, ALU.max))
                step(v.tensor_tensor(first_hot[:, :, :], hit[:, :, :], over_experts(top[:, :, :]), ALU.is_equal))
                step(v.scalar_tensor_tensor(out=rest[:, :, :], in0=first_hot[:, :, :], scalar=-3.0e38, in1=lg,
                                            op0=ALU.mult, op1=ALU.add))
                step(v.tensor_reduce(top[:, :, :], rest[:, :, :], AX.X, ALU.max))
                step(v.tensor_tensor(hit[:, :, :], rest[:, :, :], over_experts(top[:, :, :]), ALU.is_equal))
                step(v.tensor_tensor(hit[:, :, :], hit[:, :, :], over_slots(order), ALU.mult))
                step(v.tensor_reduce(top[:, :, :], hit[:, :, :], AX.X, ALU.max))
                step(v.tensor_tensor(hit[:, :, :], hit[:, :, :], over_experts(top[:, :, :]), ALU.is_equal))
                step(v.tensor_tensor(hit[:, :, :], hit[:, :, :], first_hot[:, :, :], ALU.add))
                dve.wait_ge(gate_exp, 1)
                step(v.tensor_reduce(total[:, :, :], gate_e[:, :, :], AX.X, ALU.add))
                step(v.reciprocal(total[:, :, :], total[:, :, :]))
                step(v.tensor_tensor(hit[:, :, :], hit[:, :, :], gate_e[:, :, :], ALU.mult))
                step(v.tensor_tensor(hit[:, :, :], hit[:, :, :], over_experts(total[:, :, :]), ALU.mult))
                dve.wait_ge(cw_full, 1)
                for k in range(2):
                    nc.vector.tensor_copy(cw_t[:, 4 * k:4 * k + 4, :].rearrange("p b j -> p (b j)"), banks[k][0:D, :])\
                      .then_inc(cw_copied, 1)
                nc.vector.tensor_copy(cw_tail[:, :], banks[2][0:D, 0:TXT]).then_inc(cw_copied, 1)

                with nc.vector.Fori(0, PAIRS // 2) as r:
                    for s in range(2):
                        n = 2 * r + s
                        dve.wait_ge(loaded[s], 16 * N_LOAD * (r + 1))
                        for v6 in range(UPP):
                            bp, c = divmod(v6, NCH)
                            for k in range(4):
                                dve.wait_ge(y_full, YPP * n + 4 * v6 + k + 1)
                                if s > 0 or v6 > 0:
                                    dve.wait_ge(x2_ready, ADDED + 4 * (UPP * n + v6 - 1) + max(k, 1))
                                else:
                                    dve.wait_ge(x2_ready, ADDED + 4 * UPP * n)
                                nc.vector.scalar_tensor_tensor(out=prod[:, k, :], in0=banks[4 + k % 2][:, 0:CH],
                                                               scalar=b2_sb[:, k:k + 1],
                                                               in1=cwb[s][:, k, bp, chunk[c]],
                                                               op0=ALU.add, op1=ALU.mult).then_inc(y_read, 1)

            @block.tensor
            def _(pe):
                def norm_pair(p):
                    at_least(pe, sq_done, NCH * p)
                    for c in range(NCH):
                        nc.tensor.matmul(banks[c][:, 0:CH], centre,
                                         h2_all[:, bass.ds(p, 1), chunk[c]].rearrange("p o l -> p (o l)"),
                                         start=True, stop=True).then_inc(centred, 1)
                    at_least(pe, var_read, NCH * p)
                    for c in range(NCH):
                        pe.wait_ge(sq_done, NCH * p + c + 1)
                        nc.tensor.matmul(banks[3 + c][:, 0:CH], mean, sq2[:, chunk[c]], start=True, stop=True)\
                          .then_inc(var_full, 1)
                    pe.wait_ge(x2_ready, NCH * p + NCH)
                    at_least(pe, gate_read, 2 * p)
                    for bp in range(2):
                        rows = slice(D * bp, D * bp + D)
                        for t in range(KT):
                            nc.tensor.matmul(banks[6 + bp][:, E * t:E * t + E], y2[rows, P * t:P * t + P],
                                             gate_sb[rows, :], start=True, stop=True)
                        nc.tensor.matmul(banks[6 + bp][0:TXT, E * KT:E * KT + E], y2[rows, IMG:L], gate_sb[rows, :],
                                         start=True, stop=True).then_inc(gate_full, 1)

                norm_pair(0)
                with nc.tensor.Fori(1, PAIRS) as p:
                    norm_pair(p)
                pe.wait_ge(gate_step, 17)
                for b in range(B):
                    nc.tensor.transpose(banks[b // 4][0:D, P * (b % 4):P * (b % 4) + P],
                                        hit[:, KT * b:KT * b + KT, :].rearrange("p t e -> p (t e)"), ident)
                nc.tensor.transpose(banks[2][0:D, 0:TXT], hit[0:TXT, KT * B:S72, :].rearrange("p t e -> p (t e)"),
                                    ident[0:TXT, 0:TXT])\
                  .then_inc(cw_full, 1)
                pe.wait_ge(cw_copied, 3)

                with nc.tensor.Fori(0, PAIRS // 2) as r:
                    for s in range(2):
                        n = 2 * r + s
                        pe.wait_ge(loaded[s], 16 * N_LOAD * (r + 1))

                        def experts_out(v, k):
                            pe.wait_ge(gelu_done, KPP * n + E * v + 2 * k + 2)
                            if s > 0 or 4 * v + k >= 2:
                                pe.wait_ge(y_read, YPP * n + 4 * v + k - 1)
                            for o in range(2):
                                e = 2 * k + o
                                last = nc.tensor.matmul(banks[4 + k % 2][D * o:D * o + D, 0:CH], w2_sb[:, e, :],
                                                        hid[:, e % 4, :], start=True, stop=True)
                            last.then_inc(y_full, 1)

                        for v in range(UPP):
                            bp, c = divmod(v, NCH)
                            rows = slice(D * bp, D * bp + D)
                            for k in range(4):
                                for e in (2 * k, 2 * k + 1):
                                    if s > 0 or E * v + e >= 4:
                                        pe.wait_ge(gelu_done, KPP * n + E * v + e - 3)
                                    nc.tensor.matmul(banks[e % 4][:, 0:CH], w1_sb[rows, e, :], x2[s][rows, chunk[c]],
                                                     start=True, stop=True).then_inc(hid_full, 1)
                                if k > 0:
                                    experts_out(v, k - 1)
                            experts_out(v, 3)
                            if c == NCH - 1:
                                pe.wait_ge(x2_ready, ADDED + 4 * (UPP * n + v + 1))
                                pe.wait_ge(gate_read, B + 2 * n + bp)
                                for t in range(KT):
                                    nc.tensor.matmul(banks[6][:, D * t:D * t + D], acc[:, bp, P * t:P * t + P], fold,
                                                     start=True, stop=True)
                                nc.tensor.matmul(banks[7][0:TXT, 0:D], acc[:, bp, IMG:L], fold,
                                                 start=True, stop=True).then_inc(gate_full, 1)


def constants():
    import numpy as np

    c = np.zeros((P, C_COLS), np.float32)
    i = np.arange(P)
    same = (i[:, None] // D == i[None, :] // D) / D
    c[:, C_ID:C_ID + P] = np.eye(P)
    c[:, C_CENTRE:C_CENTRE + P] = np.eye(P) - same
    c[:, C_MEAN:C_MEAN + P] = same
    c[:, C_DEN:C_DEN + P] = (i[:, None] // 32 == i[None, :] // 32) & (i[:, None] % 32 == DH)
    c[:, C_FOLD:C_FOLD + D] = i[:, None] % D == np.arange(D)[None, :]
    t = np.arange(PATCH).reshape(2, 2, 4).transpose(1, 0, 2).reshape(PATCH)
    angle = 2 * np.pi * np.arange(NFREQ)[:, None] * t[None, :] / PATCH
    c[0:NFREQ, C_DFT:C_DFT + PATCH] = np.cos(angle) / np.sqrt(PATCH)
    c[NFREQ:2 * NFREQ, C_DFT:C_DFT + PATCH] = -np.sin(angle) / np.sqrt(PATCH)
    c[:, C_ORDER:C_ORDER + E] = E - np.arange(E)
    return c


_INS = ["x", "txt", "L0_tok_W", "L0_attn_w_qkv", "L0_attn_w_proj", "L0_attn_b_proj", "L0_ffn_gate_w",
        "L0_ffn_gate_b", "L0_ffn_W1", "L0_ffn_b1", "L0_ffn_W2", "L0_ffn_b2"]


def kernel(**inputs):
    import numpy as np
    import concourse.bacc as bacc
    from concourse.bass_utils import run_bass_kernel_spmd

    nc = bacc.Bacc("TRN2", target_bir_lowering=False, num_devices=1)
    arrays = {f"in_{name}": np.ascontiguousarray(inputs[name]) for name in _INS}
    arrays["in_constants"] = constants()
    args = [nc.dram_tensor(n, a.shape, mybir.dt.from_np(a.dtype), kind="ExternalInput").ap() for n, a in arrays.items()]
    out = nc.dram_tensor("out_0", (B, L, D), F32, kind="ExternalOutput").ap()
    build(nc, *args, out)
    return run_bass_kernel_spmd(nc, [arrays], core_ids=[0]).results[0]["out_0"]
```

```python
from contextlib import ExitStack

import concourse.bass as bass
from concourse import mybir

F32 = mybir.dt.float32
BF16 = mybir.dt.bfloat16
ALU = mybir.AluOpType
ACT = mybir.ActivationFunctionType
AX = mybir.AxisListType

P = 128
B, C, T, V = 8, 64, 128, 64
TXT = 32
D = 64
PATCH, STRIDE = 16, 8
NPATCH = T // STRIDE
NFREQ = PATCH // 2 + 1
IMG = V * NPATCH
L = IMG + TXT
H, DH = 4, 16
E, HID = 8, 128
PAIRS = B // 2
CH = L // 3
NCH = 3
QTP = IMG // P + 1
LP = QTP * P
KT = IMG // P
HALF = IMG // 2
SCALE = float(DH) ** -0.5
EPS = 1e-5
ROWS = 6 * DH
UNITS = NCH * (1 + KT * H)
GROUPS = NCH * KT
QT = H * KT
MAXU = 2 * QT + 2 + NCH
PARTS = [(0, 0), (0, 1), (1, 0), (0, 2), (1, 1), (2, 0)]

C_ID, C_CENTRE, C_MEAN, C_DEN, C_FOLD, C_DFT, C_ORDER, C_TAIL = 0, 128, 256, 384, 512, 576, 592, 600
C_COLS = 632

AT_VALUES = [0, 3]
AT_RECIP = 5
AT_FINISH = [14, 17, 20, 23, 26, 29]
AT_TOKENISE = [42, 47, 50, 53, 56, 59, 62, 65, 68]
AT_REFINE = 80
FIRST_MAX = 14
AT_SHIFT = FIRST_MAX + 71
AT_PROJECT = [90, 93, 96]
PV_LAG = 2 * H

N_SETUP = 11
SHIFT_DMAS = 3
N_FFN = 8
PRESETS = 20

USES = {"tokenise": 9, "project": 3, "values": 2, "shift": 1, "finish": 6}


def build(nc, x, txt, tok_w, w_qkv, w_proj, b_proj, gate_w, gate_b, w1, b1, w2, b2, consts, out):
    with ExitStack() as ctx:
        def sb(name, shape, dt=F32):
            return ctx.enter_context(nc.sbuf_tensor(name, shape, dt))

        def bank(name):
            return ctx.enter_context(nc.psum_tensor(name, [P, 512], F32))

        def sem(name):
            return ctx.enter_context(nc.semaphore(name))

        cw_dram = nc.dram_tensor("gates_by_expert", [E, B * L], F32, kind="Internal").ap()

        cst = sb("cst", [P, C_COLS])
        ident = cst[:, C_ID:C_ID + P]
        centre = cst[:, C_CENTRE:C_CENTRE + P]
        mean = cst[:, C_MEAN:C_MEAN + P]
        den_sel = cst[:, C_DEN:C_DEN + P]
        fold = cst[:, C_FOLD:C_FOLD + D]
        qkv_in = sb("qkv_in", [P, 2, D])
        v_in = sb("v_in", [D, 2, D])
        proj_in = sb("proj_in", [D, H, 32])
        qkT = sb("qkT", [P, P])
        vT = sb("vT", [P, 2, D])
        projT = sb("projT", [P, D])
        proj_bias = sb("proj_bias", [P, 1])
        gate_sb = sb("gate_sb", [P, E])
        gate_bias = sb("gate_bias", [P, E])
        w1_sb = sb("w1_sb", [P, E, HID])
        w2_sb = sb("w2_sb", [P, E, D])
        biases = sb("biases", [P, E + E // 2])
        b1_sb, b2_sb = biases[:, 0:E], biases[:, E:E + E // 2]
        bias_in = sb("bias_in", [E + E // 2, P])
        tok_m = sb("tok_m", [P, 8, D])
        h2_all = sb("h2_all", [P, PAIRS, L])

        banks = [bank(f"bank{i}") for i in range(8)]
        score_bank = banks[0:3]
        o_bank = banks[3]
        max_bank = banks[4:7]
        side_bank = banks[7]

        setup_loaded = sem("setup_loaded")
        ffn_loaded = sem("ffn_loaded")
        preset = sem("preset")
        setup_psum = sem("setup_psum")
        setup_done = sem("setup_done")
        x_loaded = sem("x_loaded")
        side_full = sem("side_full")
        side_free = sem("side_free")
        rstd_act = sem("rstd_act")
        rstd_dve = sem("rstd_dve")
        xn_ready = sem("xn_ready")
        h_copied = sem("h_copied")
        h_stored = sem("h_stored")
        part1_done = sem("part1_done")
        part2_done = sem("part2_done")
        part3_done = sem("part3_done")
        stacked = sem("stacked")
        v_ready = sem("v_ready")
        max_scores = sem("max_scores")
        max_done = sem("max_done")
        neg_max = sem("neg_max")
        shift_step = sem("shift_step")
        shifted = sem("shifted")
        scores_ready = sem("scores_ready")
        exp_done = sem("exp_done")
        pv_done = sem("pv_done")
        o_ready = sem("o_ready")
        o_free = sem("o_free")
        den_moved = sem("den_moved")
        recip_done = sem("recip_done")
        recip_moved = sem("recip_moved")
        on_ready = sem("on_ready")

        phase1 = ExitStack()

        def sb1(name, shape, dt=F32):
            return phase1.enter_context(nc.sbuf_tensor(name, shape, dt))

        xt = [sb1(f"x{i}", [P, NPATCH + 1, 4, V]) for i in range(2)]
        text_in = sb1("text_in", [TXT, 2, D])
        h_new = sb1("h_new", [P, L])
        h_res = sb1("h_res", [P, L])
        xc = sb1("xc", [P, L])
        sq = sb1("sq", [P, L])
        var = sb1("var", [P, L])
        rstd = sb1("rstd", [P, L])
        rstd_sq = sb1("rstd_sq", [P, L])
        xn = sb1("xn", [P, L])
        qk_part = [sb1(f"qk_part{i}", [P, L], BF16) for i in range(3)]
        qk_rest = sb1("qk_rest", [P, L])
        qs = [sb1(f"q_stack{i}", [P, H, LP], BF16) for i in range(2)]
        ks = [sb1(f"k_stack{i}", [P, H, LP], BF16) for i in range(2)]
        v_tiles = [sb1(f"v_tiles{i}", [P, KT, H, 32]) for i in range(2)]
        v_tail = [sb1(f"v_tail{i}", [P, P]) for i in range(2)]
        max_parts = sb1("max_parts", [P, QT, 3])
        max_tail = sb1("max_tail", [P, NCH])
        negm = sb1("negm", [P, 2, P])
        m_part = sb1("m_part", [H * QTP, 3, P], BF16)
        m_rest = sb1("m_rest", [H * QTP, P])
        probs = sb1("probs", [P, 3, H, CH])
        tok_in = probs[0:2 * NFREQ, :, :, :].rearrange("r i h l -> r (i h l)")[:, 0:D * C]\
            .rearrange("r (d c) -> r d c", c=C)
        probs_tail = [sb1(f"probs_tail{i}", [P, CH]) for i in range(NCH)]
        ot = [sb1(f"heads_out{i}", [P, L]) for i in range(2)]
        den = sb1("den", [P, H * L // P])
        recip_rows = sb1("recip_rows", [P, L])
        recip = sb1("recip", [P, L])
        on = sb1("on", [P, L])

        g_values0 = USES["tokenise"] + USES["project"]
        g_project1 = g_values0 + USES["values"]
        g_shift0 = g_project1 + USES["project"]
        g_slot0 = g_shift0 + 1
        per_slot = USES["values"] + USES["finish"] + USES["shift"] + USES["project"]
        g_slot1 = g_slot0 + per_slot - USES["finish"] + USES["tokenise"]
        per_round = 2 * per_slot + USES["tokenise"]

        def slot_plan(odd, q):
            return (2 * q + 1, g_slot1 + per_round * q) if odd else (2 * q + 2, g_slot1 + per_slot + per_round * q)

        def side_steps(u, stages, b, par, q, g):
            ahead = q + 1 if par else q + 2
            order = []
            if u == 0:
                for i in range(2):
                    if "finish" in stages:
                        order.append(("spread", i, b - 1, 1 - par, q, g))
                    if "values" in stages:
                        order.append(("stack", i, b + 1, 1 - par, q + 1, g))
            if u == AT_RECIP and "finish" in stages:
                order.append(("recip", 0, b - 1, 1 - par, q, g))
            if u == AT_REFINE and "tokenise" in stages:
                order.append(("refine", 0, None, None, q + 2, g))
            if u == 0 and "load" in stages:
                order.append(("load", 0, None, None, q + 2, g))
            for stage, at, t, tpar, pair in (("values", AT_VALUES, b + 1, 1 - par, q + 1),
                                             ("finish", AT_FINISH, b - 1, 1 - par, q),
                                             ("tokenise", AT_TOKENISE, None, None, q + 2),
                                             ("shift", [AT_SHIFT], b + 1, 1 - par, q + 1),
                                             ("project", AT_PROJECT, b + 2, par, ahead)):
                if stage in stages:
                    if u in at:
                        order.append((stage, at.index(u), t, tpar, pair, g))
                    if stage == "tokenise":
                        for i in range(2):
                            if AT_TOKENISE[i] - 4 < u < AT_TOKENISE[i]:
                                order.append(("embed", (i, u - AT_TOKENISE[i] + 3), None, None, pair, g))
                    g = g + USES[stage]
            if "maxima" in stages and FIRST_MAX <= u < FIRST_MAX + MAXU:
                order.append(("maxima", u - FIRST_MAX, b + 1, 1 - par, q + 1, g))
            return order

        NEXT = ("values", "maxima", "shift")
        BESIDE = {0: NEXT + ("project", "tokenise"), "odd": NEXT + ("load", "project", "finish"),
                  "even": NEXT + ("project", "finish", "tokenise"), 5: NEXT + ("project", "finish"),
                  6: NEXT + ("finish",), 7: ("finish",)}

        def run_phase1(eng, attend_unit, side, after_slot):
            def slot(b, par, q, g, stages):
                for u in range(UNITS):
                    attend_unit(b, par, u, g)
                    for step in side_steps(u, stages, b, par, q, g):
                        side(*step)
                after_slot(b, par)

            for i in range(USES["tokenise"]):
                for j in range(3 if i < 2 else 0):
                    side("embed", (i, j), None, None, 0, 0)
                side("tokenise", i, None, None, 0, 0)
            side("refine", 0, None, None, 0, 0)
            for i in range(USES["project"]):
                side("project", i, 0, 0, 0, USES["tokenise"])
            for i in range(2):
                side("stack", i, 0, 0, 0, 0)
            for i in range(USES["values"]):
                side("values", i, 0, 0, 0, g_values0)
            for u in range(MAXU):
                side("maxima", u, 0, 0, 0, g_project1)
                if u in (12, 24, 36):
                    side("project", u // 12 - 1, 1, 1, 0, g_project1)
            side("shift", 0, 0, 0, 0, g_shift0)
            slot(0, 0, -1, g_slot0, BESIDE[0])
            with eng.Fori(0, 2) as q:
                b, g = slot_plan(True, q)
                slot(b, 1, q, g, BESIDE["odd"])
                b, g = slot_plan(False, q)
                slot(b, 0, q, g, BESIDE["even"])
            b, g = slot_plan(True, 2)
            slot(b, 1, 2, g, BESIDE[5])
            slot(6, 0, 2, g + per_slot, BESIDE[6])
            g7 = g + 2 * per_slot - USES["project"]
            slot(7, 1, 3, g7, BESIDE[7])
            for stage, i in (("spread", 0), ("recip", 0), ("spread", 1)):
                side(stage, i, 7, 1, 3, g7)
            for i in range(USES["finish"]):
                side("finish", i, 7, 1, 3, g7 + USES["finish"])

        def at_least(eng, s, value):
            if not isinstance(value, int) or value > 0:
                eng.wait_ge(s, value)

        def full(eng, i, g):
            eng.wait_ge(side_full, g + i + 1)
            return side_bank

        def freed(eng, i, g):
            at_least(eng, side_free, g + i + 1)

        X_DMAS = 9
        chunk = [slice(c * CH, (c + 1) * CH) for c in range(NCH)]

        def guess_rstd(act, var, rstd, rstd_sq, n, done):
            nc.scalar.activation(rstd_sq[:, :], var[:, :], ACT.Ln).then_inc(done, 1)
            act.wait_ge(done, 3 * n + 1)
            nc.scalar.activation(rstd[:, :], rstd_sq[:, :], ACT.Exp, scale=-0.5).then_inc(done, 1)
            act.wait_ge(done, 3 * n + 2)
            nc.scalar.activation(rstd_sq[:, :], rstd[:, :], ACT.Square).then_inc(done, 1)

        def refine_rstd(dve, var, rstd, rstd_sq, c, n, guessed, done):
            dve.wait_ge(guessed, 3 * n + 3)
            nc.vector.scalar_tensor_tensor(out=rstd_sq[:, chunk[c]], in0=var[:, chunk[c]], scalar=-0.5,
                                           in1=rstd_sq[:, chunk[c]], op0=ALU.mult, op1=ALU.mult).then_inc(done, 1)
            dve.wait_ge(done, 2 * (NCH * n + c) + 1)
            nc.vector.scalar_tensor_tensor(out=rstd[:, chunk[c]], in0=rstd_sq[:, chunk[c]], scalar=1.5,
                                           in1=rstd[:, chunk[c]], op0=ALU.add, op1=ALU.mult).then_inc(done, 1)

        with nc.Block() as block:

            @block.sync
            def _(sp):
                def load_x(pair):
                    for bp in range(2):
                        src = x[bass.ds(2 * pair + bp, 1)].rearrange("o c t v -> (o c) t v")
                        for th in range(2):
                            part = slice(C * th, C * th + C)
                            sp.dma_start(xt[bp][part, 0:NPATCH, :, :],
                                         src.rearrange("c (j h t) v -> h c j t v", h=2, t=4)[th])\
                              .then_inc(x_loaded, 16)
                            sp.dma_start(xt[bp][part, NPATCH, :, :],
                                         src[:, T - 1:T, :].broadcast_to([C, 4, V])).then_inc(x_loaded, 16)
                    sp.dma_start(text_in[:, :, :], txt[bass.ds(2 * pair, 2)].rearrange("b t d -> t b d"))\
                      .then_inc(x_loaded, 16)

                sp.dma_start(cst[:, :], consts).then_inc(setup_loaded, 16)
                sp.dma_start(tok_in[:, :, :], tok_w.rearrange("d (r c) -> r d c", c=C)).then_inc(setup_loaded, 16)
                for s in range(2):
                    for half in range(2):
                        sp.dma_start(qkv_in[D * s:D * s + D, half, :],
                                     w_qkv[D * s:D * s + D, :].rearrange("(h d) c -> d h c", h=H))\
                          .then_inc(setup_loaded, 16)
                for half in range(2):
                    sp.dma_start(v_in[:, half, :], w_qkv[2 * D:3 * D, :]).then_inc(setup_loaded, 16)
                sp.dma_start(bias_in[0:E, :], b1).then_inc(setup_loaded, 16)
                sp.dma_start(bias_in[E:E + E // 2, :], b2.rearrange("(k o) n -> k (o n)", o=2))\
                  .then_inc(setup_loaded, 16)
                sp.wait_ge(preset, 1)
                sp.dma_start(proj_in[:, :, 0:DH], w_proj.rearrange("n (h d) -> n h d", h=H)).then_inc(setup_loaded, 16)
                load_x(0)
                for half in range(2):
                    rows = slice(D * half, D * half + D)
                    sp.dma_start(proj_bias[rows, :], b_proj.rearrange("(n o) -> n o", o=1)).then_inc(ffn_loaded, 16)
                    sp.dma_start(gate_sb[rows, :], gate_w).then_inc(ffn_loaded, 16)
                    sp.dma_start(w1_sb[rows, :, :], w1.rearrange("e c n -> c e n")).then_inc(ffn_loaded, 16)
                sp.dma_start(gate_bias[:, :], gate_b.rearrange("(o e) -> o e", o=1).broadcast_to([P, E]))\
                  .then_inc(ffn_loaded, 16)
                sp.dma_start(w2_sb[:, :, :], w2.rearrange("e n c -> n e c")).then_inc(ffn_loaded, 16)

                def stack_parts(par, products):
                    for n in products:
                        a, k = PARTS[n]
                        rows = slice(DH * n, DH * n + DH)
                        sp.dma_start(qs[par][rows, :, 0:L], qk_part[a][0:D, :]).then_inc(stacked, 16)
                        sp.dma_start(ks[par][rows, :, 0:L], qk_part[k][D:P, :]).then_inc(stacked, 16)

                def attend_unit(b, par, u, g):
                    pass

                def side(stage, i, t, par, pair, g):
                    if (stage, i) == ("spread", 0):
                        sp.wait_ge(o_free, NCH * (t + 1))
                        sp.dma_start(den[:, :], ot[par][DH:P:32, :]).then_inc(den_moved, 16)
                    elif stage == "spread":
                        sp.wait_ge(recip_done, t + 1)
                        sp.dma_start(recip_rows[DH:P:32, :], den[:, :]).then_inc(recip_moved, 16)
                    elif (stage, i) == ("stack", 0):
                        attended, split = UNITS * (t - 1), NCH * (t + 1)
                        at_least(sp, scores_ready, attended)
                        sp.wait_ge(part1_done, split)
                        sp.wait_ge(part2_done, split)
                        sp.wait_ge(part3_done, split)
                        stack_parts(par, range(3))
                    elif stage == "stack":
                        stack_parts(par, range(3, 6))
                    elif stage == "shift":
                        sp.wait_ge(shift_step, 3 * (t + 1))
                        for n in range(3):
                            row = slice(ROWS + n, ROWS + n + 1)
                            sp.dma_start(qs[par][row, :, :], m_part[:, n, :]).then_inc(shifted, 16)
                    elif stage == "load":
                        sp.wait_ge(xn_ready, pair)
                        load_x(pair)
                    elif stage == "tokenise" and isinstance(pair, int) and pair == 0 and i == 2:
                        sp.wait_ge(side_full, 3)
                        load_x(1)
                    elif stage == "tokenise" and isinstance(pair, int) and pair == 0 and i == 3:
                        freed(sp, 2, g)
                        sp.dma_start(h_res[:, :], h_new[:, :]).then_inc(h_copied, 16)
                    elif stage == "finish" and i == 5 and par == 1:
                        freed(sp, 5, g)
                        sp.dma_start(h2_all[:, bass.ds(pair, 1), :].rearrange("p o l -> p (o l)"), h_res[:, :])\
                          .then_inc(h_stored, 16)
                        sp.wait_ge(h_stored, 16 * (pair + 1))
                        if not (isinstance(t, int) and t == B - 1):
                            sp.wait_ge(xn_ready, pair + 2)
                            sp.dma_start(h_res[:, :], h_new[:, :]).then_inc(h_copied, 16)

                run_phase1(nc.sync, attend_unit, side, lambda b, par: None)
                sp.wait_ge(ffn_loaded, 16 * N_FFN)

            @block.gpsimd
            def _(pool):
                def side(stage, i, t, par, pair, g):
                    if stage == "refine":
                        for c in range(NCH):
                            pool.wait_ge(rstd_dve, 2 * (NCH * pair + c + 1))
                            last = nc.gpsimd.tensor_tensor(xn[:, chunk[c]], xc[:, chunk[c]], rstd[:, chunk[c]], ALU.mult)
                        last.then_inc(xn_ready, 1)
                    elif stage == "project":
                        pool.wait_ge(part2_done, NCH * t + i + 1)
                        at_least(pool, stacked, 16 * 12 * t)
                        nc.gpsimd.tensor_tensor(qk_part[2][:, chunk[i]], qk_rest[:, chunk[i]], qk_part[1][:, chunk[i]],
                                                ALU.subtract).then_inc(part3_done, 1)
                    elif stage == "finish" and i % 2 == 0:
                        freed(pool, i, g)
                        c = i // 2
                        nc.gpsimd.tensor_tensor(on[:, chunk[c]], ot[par][:, chunk[c]], recip[:, chunk[c]], ALU.mult)\
                          .then_inc(on_ready, 1)

                run_phase1(nc.gpsimd, lambda b, par, u, g: None, side, lambda b, par: None)

            @block.scalar
            def _(act):
                act.wait_ge(setup_psum, 1)
                nc.scalar.activation(qkT[:, :], banks[0][:, 0:P], ACT.Copy)
                act.wait_ge(preset, 2)
                for i in range(2):
                    rows = slice(D * i, D * i + D)
                    nc.scalar.activation(vT[rows, i, :], banks[0][rows, P:P + D], ACT.Copy)
                nc.scalar.activation(biases[:, :], banks[0][:, 2 * P:2 * P + E + E // 2], ACT.Copy)
                nc.scalar.activation(projT[:, :], banks[0][:, P + D:P + 2 * D], ACT.Copy).then_inc(setup_done, 1)

                def evacuate_o(b, par, qc):
                    act.wait_ge(o_ready, NCH * b + qc + 1)
                    nc.scalar.activation(ot[par][:, chunk[qc]], o_bank[:, 0:CH], ACT.Copy).then_inc(o_free, 1)

                def attend_unit(b, par, u, g):
                    qc, r = divmod(u, 1 + KT * H)
                    act.wait_ge(scores_ready, UNITS * b + u + 1)
                    src = score_bank[u % 3][:, 0:CH]
                    if r == 0:
                        nc.scalar.activation(probs_tail[qc][:, :], src, ACT.Exp, scale=SCALE).then_inc(exp_done, 1)
                        return
                    kt, h = divmod(r - 1, H)
                    group = KT * qc + kt
                    if h == 0:
                        at_least(act, pv_done, GROUPS * b + group - 2)
                    nc.scalar.activation(probs[:, group % 3, h, :], src, ACT.Exp, scale=SCALE).then_inc(exp_done, 1)
                    if r == 6 and qc > 0:
                        evacuate_o(b, par, qc - 1)

                def side(stage, i, t, par, pair, g):
                    if stage == "project":
                        bank = full(act, i, g)
                        at_least(act, stacked, 16 * 12 * t)
                        nc.scalar.activation(qk_part[0][:, chunk[i]], bank[:, 0:CH], ACT.Copy).then_inc(part1_done, 1)
                    elif stage == "values":
                        bank = full(act, i, g)
                        if i == 0:
                            nc.scalar.activation(v_tiles[par][:, :, :, 0:DH].rearrange("p k h d -> p (k h) d"),
                                                 bank[:, :].rearrange("p (k d) -> p k d", d=DH), ACT.Copy)\
                              .then_inc(side_free, 1)
                        else:
                            for h in range(H):
                                rows = slice(32 * h, 32 * h + 32)
                                last = nc.scalar.activation(v_tail[par][rows, 32 * h:32 * h + DH], bank[rows, 0:DH], ACT.Copy)
                            last.then_inc(side_free, 1)
                    elif stage == "tokenise" and i in (0, 2):
                        bank = full(act, i, g)
                        at_least(act, h_copied, 16 * pair)
                        cols, n = (slice(0, HALF), HALF) if i == 0 else (slice(IMG, L), TXT)
                        nc.scalar.activation(h_new[:, cols], bank[:, 0:n], ACT.Copy).then_inc(side_free, 1)
                    elif stage == "tokenise" and 3 <= i < 6:
                        c = i - 3
                        bank = full(act, i, g)
                        nc.scalar.activation(xc[:, chunk[c]], bank[:, 0:CH], ACT.Copy)
                        nc.scalar.activation(sq[:, chunk[c]], bank[:, 0:CH], ACT.Square).then_inc(side_free, 1)
                    elif stage == "finish" and i % 2 == 0:
                        bank = full(act, i, g)
                        nc.scalar.activation(recip[:, chunk[i // 2]], bank[:, 0:CH], ACT.Copy).then_inc(side_free, 1)
                    elif stage == "tokenise" and i == 8:
                        freed(act, 8, g)
                        guess_rstd(act, var, rstd, rstd_sq, pair, rstd_act)

                run_phase1(nc.scalar, attend_unit, side, lambda b, par: evacuate_o(b, par, NCH - 1))

            @block.vector
            def _(dve):
                nc.vector.memset(proj_in[:, :, :], 0.0).then_inc(preset, 1)
                nc.vector.memset(vT[:, :, :], 0.0).then_inc(preset, 1)
                for i in range(2):
                    nc.vector.memset(v_tiles[i][:, :, :, :], 0.0).then_inc(preset, 1)
                    nc.vector.memset(v_tail[i][:, :], 0.0).then_inc(preset, 1)
                    nc.vector.memset(ks[i][ROWS:ROWS + 3, :, :], 1.0).then_inc(preset, 1)
                nc.vector.memset(negm[:, :, :], 0.0).then_inc(preset, 1)
                nc.vector.memset(recip_rows[:, :], 0.0).then_inc(preset, 1)
                dve.wait_ge(preset, 10)
                for i in range(2):
                    nc.vector.memset(v_tiles[i][:, :, :, DH:DH + 1], 1.0).then_inc(preset, 1)
                    for h in range(H):
                        nc.vector.memset(v_tail[i][32 * h:32 * h + 32, 32 * h + DH:32 * h + DH + 1], 1.0)\
                          .then_inc(preset, 1)
                dve.wait_ge(setup_psum, 2)
                nc.vector.tensor_copy(tok_m[:, :, :].rearrange("p k d -> p d k"),
                                      banks[1][:, :].rearrange("p (d k) -> p d k", k=8)).then_inc(setup_done, 1)

                def side(stage, i, t, par, pair, g):
                    if stage == "recip":
                        dve.wait_ge(den_moved, 16 * (t + 1))
                        nc.vector.reciprocal(den[:, :], den[:, :]).then_inc(recip_done, 1)
                    elif stage == "refine":
                        for c in range(NCH):
                            refine_rstd(dve, var, rstd, rstd_sq, c, pair, rstd_act, rstd_dve)
                    elif stage == "maxima":
                        n = MAXU * t + i
                        dve.wait_ge(max_scores, n + 1)
                        src = max_bank[i % 3]
                        if i < 2 * QT:
                            nc.vector.tensor_reduce(max_parts[:, i // 2, i % 2:i % 2 + 1], src[:, :], AX.X, ALU.max)\
                              .then_inc(max_done, 1)
                        elif i < 2 * QT + 2:
                            part = slice(16 * (i - 2 * QT), 16 * (i - 2 * QT) + 16)
                            nc.vector.tensor_reduce(max_parts[:, part, 2],
                                                    src[:, :].rearrange("p (n k) -> p n k", k=TXT), AX.X, ALU.max)\
                              .then_inc(max_done, 1)
                        else:
                            c = i - 2 * QT - 2
                            nc.vector.tensor_reduce(max_tail[:, c:c + 1], src[:, 0:CH], AX.X, ALU.max)\
                              .then_inc(max_done, 1)
                        if i == MAXU - 1:
                            dve.wait_ge(max_done, MAXU * (t + 1))
                            nc.vector.tensor_reduce(
                                negm[:, 0, 0:H * QTP].rearrange("p (h k) -> p h k", h=H)[:, :, 0:KT],
                                max_parts[:, :, :].rearrange("p (h k) n -> p h k n", h=H), AX.X, ALU.max, negate=True)
                            for h in range(H):
                                rows, col = slice(32 * h, 32 * h + 32), QTP * h + KT
                                last = nc.vector.tensor_reduce(negm[rows, 1, col:col + 1], max_tail[rows, :],
                                                               AX.X, ALU.max, negate=True)
                            last.then_inc(neg_max, 1)
                    elif stage == "shift":
                        bank = full(dve, 0, g)
                        at_least(dve, shifted, 16 * SHIFT_DMAS * t)
                        src = bank[0:H * QTP, 0:P]
                        nc.vector.tensor_copy(m_part[:, 0, :], src).then_inc(shift_step, 1)
                        dve.wait_ge(shift_step, 3 * t + 1)
                        nc.vector.tensor_tensor(m_rest[:, :], src, m_part[:, 0, :], ALU.subtract)\
                          .then_inc(side_free, 1)
                        freed(dve, 0, g)
                        nc.vector.tensor_copy(m_part[:, 1, :], m_rest[:, :]).then_inc(shift_step, 1)
                        dve.wait_ge(shift_step, 3 * t + 2)
                        nc.vector.tensor_tensor(m_part[:, 2, :], m_rest[:, :], m_part[:, 1, :], ALU.subtract)\
                          .then_inc(shift_step, 1)
                    elif stage == "project":
                        dve.wait_ge(part1_done, NCH * t + i + 1)
                        at_least(dve, part3_done, NCH * t)
                        at_least(dve, stacked, 16 * 12 * t)
                        nc.vector.tensor_tensor(qk_rest[:, chunk[i]], side_bank[:, 0:CH], qk_part[0][:, chunk[i]],
                                                ALU.subtract).then_inc(side_free, 1)
                        freed(dve, i, g)
                        nc.vector.tensor_copy(qk_part[1][:, chunk[i]], qk_rest[:, chunk[i]]).then_inc(part2_done, 1)
                    elif stage == "tokenise" and i == 1:
                        bank = full(dve, i, g)
                        at_least(dve, h_copied, 16 * pair)
                        nc.vector.tensor_copy(h_new[:, HALF:IMG], bank[:, :]).then_inc(side_free, 1)
                    elif stage == "tokenise" and i >= 6:
                        c = i - 6
                        bank = full(dve, i, g)
                        nc.vector.tensor_scalar(var[:, chunk[c]], bank[:, 0:CH], EPS, None, ALU.add).then_inc(side_free, 1)
                    elif stage == "finish":
                        c = i // 2
                        if i % 2 == 1:
                            bank = full(dve, i, g)
                            rows = slice(D * par, D * par + D)
                            dve.wait_ge(h_copied, 16 * (pair + 1))
                            dve.wait_ge(ffn_loaded, 16 * N_FFN)
                            nc.vector.scalar_tensor_tensor(out=h_res[rows, chunk[c]], in0=bank[rows, 0:CH],
                                                           scalar=proj_bias[rows, :], in1=h_res[rows, chunk[c]],
                                                           op0=ALU.add, op1=ALU.add).then_inc(side_free, 1)

                run_phase1(nc.vector, lambda b, par, u, g: None, side, lambda b, par: None)

            @block.tensor
            def _(pe):
                pe.wait_ge(setup_loaded, 16 * N_SETUP)
                nc.tensor.transpose(banks[0][:, 0:P], qkv_in[:, :, :].rearrange("p a c -> p (a c)"), ident)
                nc.tensor.transpose(banks[0][:, P:P + D], v_in[:, :, :].rearrange("p a c -> p (a c)"), ident[0:D, 0:D])
                nc.tensor.transpose(banks[0][:, P + D:P + 2 * D], proj_in[:, :, :].rearrange("p h d -> p (h d)"),
                                    ident[0:D, 0:D])
                nc.tensor.transpose(banks[0][:, 2 * P:2 * P + E + E // 2], bias_in[:, :],
                                    ident[0:E + E // 2, 0:E + E // 2]).then_inc(setup_psum, 1)
                for d in range(D):
                    for th in range(2):
                        last = nc.tensor.matmul(banks[1][C * th:C * th + C, 8 * d:8 * d + 8], tok_in[:, d, :],
                                                cst[0:2 * NFREQ, C_DFT + 8 * th:C_DFT + 8 * th + 8],
                                                start=True, stop=True)
                last.then_inc(setup_psum, 1)
                pe.wait_ge(setup_done, 2)
                pe.wait_ge(preset, PRESETS)

                def heads_times_v(b, par, group, g):
                    qc, kt = divmod(group, KT)
                    pe.wait_ge(exp_done, UNITS * b + (1 + KT * H) * qc + 1 + H * kt + H)
                    if kt == 0:
                        at_least(pe, o_free, NCH * b + qc)
                        if qc == 0:
                            pe.wait_ge(side_free, g)
                    for h in range(H):
                        last = nc.tensor.matmul(o_bank[32 * h:32 * h + 32, 0:CH], v_tiles[par][:, kt, h, :],
                                                probs[:, group % 3, h, :], start=(kt == 0), stop=False,
                                                skip_group_check=True)
                    last.then_inc(pv_done, 1)
                    if kt == KT - 1:
                        nc.tensor.matmul(o_bank[:, 0:CH], v_tail[par][:, :], probs_tail[qc][:, :], start=False, stop=True,
                                         skip_group_check=True).then_inc(o_ready, 1)

                def attend_unit(b, par, u, g):
                    qc, r = divmod(u, 1 + KT * H)
                    if u == 0:
                        pe.wait_ge(shifted, 16 * SHIFT_DMAS * (b + 1))
                    at_least(pe, exp_done, UNITS * b + u - 2)
                    bank = score_bank[u % 3]
                    if r == 0:
                        for h in range(H):
                            last = nc.tensor.matmul(bank[32 * h:32 * h + 32, 0:CH], ks[par][0:ROWS + 3, h, IMG:L],
                                                    qs[par][0:ROWS + 3, h, chunk[qc]], start=True, stop=True)
                    else:
                        kt, h = divmod(r - 1, H)
                        last = nc.tensor.matmul(bank[:, 0:CH], ks[par][0:ROWS + 3, h, P * kt:P * kt + P],
                                                qs[par][0:ROWS + 3, h, chunk[qc]], start=True, stop=True)
                    last.then_inc(scores_ready, 1)
                    chunk_of, step = divmod(u - PV_LAG, 1 + KT * H)
                    if chunk_of >= 0 and step % H == 0 and step < H * KT:
                        heads_times_v(b, par, KT * chunk_of + step // H, g)

                def embed(half, part):
                    for k in (2 * part, 2 * part + 1):
                        next_block, t4 = divmod(k, 4)
                        first = NPATCH // 2 * half + next_block
                        for bp in range(2):
                            last = nc.tensor.matmul(side_bank[D * bp:D * bp + D, :], tok_m[:, k, :],
                                                    xt[bp][:, first:first + NPATCH // 2, t4, :],
                                                    start=(k == 0), stop=(k == 7), skip_group_check=True)
                    return last

                def side(stage, i, t, par, pair, g):
                    rows = None if par is None else slice(D * par, D * par + D)
                    if stage == "maxima":
                        n = MAXU * t + i
                        if i == 0:
                            pe.wait_ge(stacked, 16 * 12 * (t + 1))
                        at_least(pe, max_done, n - 2)
                        bank = max_bank[i % 3]
                        if i < 2 * QT:
                            h, qt = divmod(i // 2, KT)
                            last = nc.tensor.matmul(bank[:, :], qs[par][0:ROWS, h, P * qt:P * qt + P],
                                                    ks[par][0:ROWS, h, HALF * (i % 2):HALF * (i % 2) + HALF],
                                                    start=True, stop=True)
                        elif i < 2 * QT + 2:
                            for j in range(16):
                                h, qt = divmod(16 * (i - 2 * QT) + j, KT)
                                last = nc.tensor.matmul(bank[:, TXT * j:TXT * j + TXT], qs[par][0:ROWS, h, P * qt:P * qt + P],
                                                        ks[par][0:ROWS, h, IMG:L], start=True, stop=True)
                        else:
                            c = i - 2 * QT - 2
                            for h in range(H):
                                last = nc.tensor.matmul(bank[32 * h:32 * h + 32, 0:CH], qs[par][0:ROWS, h, IMG:L],
                                                        ks[par][0:ROWS, h, chunk[c]], start=True, stop=True)
                        last.then_inc(max_scores, 1)
                        return
                    if stage == "embed":
                        half, part = i
                        if part == 0:
                            if half == 0:
                                pe.wait_ge(x_loaded, 16 * X_DMAS * (pair + 1))
                            freed(pe, half - 1, g)
                        embed(half, part)
                        return
                    if stage in ("spread", "stack", "load", "recip", "refine"):
                        return
                    bank = side_bank
                    freed(pe, i - 1, g)
                    if stage == "shift":
                        pe.wait_ge(neg_max, t + 1)
                        nc.tensor.matmul(bank[:, 0:P], negm[:, 0, :], ident, start=True, stop=False,
                                         skip_group_check=True)
                        last = nc.tensor.matmul(bank[:, 0:TXT], negm[:, 1, :], cst[:, C_TAIL:C_TAIL + TXT],
                                                start=False, stop=True, skip_group_check=True)
                    elif stage == "project":
                        if i == 0:
                            pe.wait_ge(xn_ready, pair + 1)
                        last = nc.tensor.matmul(bank[:, 0:CH], qkT[rows, :], xn[rows, chunk[i]], start=True, stop=True)
                    elif stage == "values":
                        if i == 0:
                            for tile in range(KT):
                                last = nc.tensor.matmul(bank[:, D * tile:D * tile + D], xn[:, P * tile:P * tile + P],
                                                        vT[:, par, :], start=True, stop=True)
                        else:
                            for h in range(H):
                                last = nc.tensor.matmul(bank[32 * h:32 * h + 32, 0:DH], xn[:, IMG:L],
                                                        vT[:, par, DH * h:DH * h + DH], start=True, stop=True)
                    elif stage == "tokenise":
                        if i < 2:
                            last = embed(i, 3)
                        elif i == 2:
                            last = nc.tensor.matmul(bank[:, 0:TXT], text_in[:, :, :].rearrange("t b d -> t (b d)"),
                                                    ident[0:TXT, 0:TXT], start=True, stop=True)
                        elif i < 6:
                            last = nc.tensor.matmul(bank[:, 0:CH], centre, h_new[:, chunk[i - 3]], start=True, stop=True)
                        else:
                            freed(pe, i - 3, g)
                            last = nc.tensor.matmul(bank[:, 0:CH], mean, sq[:, chunk[i - 6]], start=True, stop=True)
                    elif stage == "finish":
                        c = i // 2
                        if i == 0:
                            pe.wait_ge(recip_moved, 16 * (t + 1))
                        if i % 2 == 0:
                            last = nc.tensor.matmul(bank[:, 0:CH], den_sel, recip_rows[:, chunk[c]], start=True, stop=True)
                        else:
                            pe.wait_ge(on_ready, NCH * t + c + 1)
                            last = nc.tensor.matmul(bank[rows, 0:CH], projT[:, :], on[:, chunk[c]], start=True, stop=True)
                    last.then_inc(side_full, 1)

                run_phase1(nc.tensor, attend_unit, side, lambda b, par: heads_times_v(b, par, GROUPS - 1, None))

        phase1.close()

        y2 = sb("x2_now", [P, L])
        x2_all = sb("x2_all", [P, PAIRS, L])
        xc2, sq2, var2 = sb("xc2", [P, L]), sb("sq2", [P, L]), sb("var2", [P, L])
        rstd2, rstd2_sq = sb("rstd2", [P, L]), sb("rstd2_sq", [P, L])
        S72 = B * (KT + 1)
        logits = sb("logits", [P, S72, E])
        gate_e = sb("gate_e", [P, S72, E])
        rest = sb("rest", [P, S72, E])
        hit = sb("hit", [P, S72, E])
        first_hot = sb("first_hot", [P, S72, E])
        top = sb("top", [P, S72, 1])
        total = sb("total", [P, S72, 1])
        cw_t = sb("cw_t", [D, B, P])
        cw_tail = sb("cw_tail", [D, TXT])
        x2 = [sb(f"x2_{i}", [P, L]) for i in range(2)]
        h2 = [sb(f"h2_{i}", [P, L]) for i in range(2)]
        cwb = [sb(f"cwb{i}", [P, E // 2, 2, L]) for i in range(2)]
        hid = sb("hid", [P, 4, CH])
        prod = sb("prod", [P, 4, CH])
        acc = sb("acc", [P, 2, L])
        outs = [[sb(f"outs{i}{j}", [P, KT, D]) for j in range(2)] for i in range(2)]
        out_tail = [[sb(f"out_tail{i}{j}", [TXT, D]) for j in range(2)] for i in range(2)]

        centred = sem("centred")
        sq_done = sem("sq_done")
        var_full = sem("var_full")
        var_read = sem("var_read")
        rstd2_act = sem("rstd2_act")
        rstd2_dve = sem("rstd2_dve")
        x2_ready = sem("x2_ready")
        x2_stored = sem("x2_stored")
        gate_full = sem("gate_full")
        gate_read = sem("gate_read")
        gate_step = sem("gate_step")
        gate_exp = sem("gate_exp")
        cw_full = sem("cw_full")
        cw_copied = sem("cw_copied")
        cw_stored = sem("cw_stored")
        loaded = [sem("loaded0"), sem("loaded1")]
        hid_full = sem("hid_full")
        gelu_done = sem("gelu_done")
        y_full = sem("y_full")
        y_read = sem("y_read")
        out_stored = sem("out_stored")
        zeroed = sem("zeroed")

        UPP = 2 * NCH
        KPP = UPP * E
        YPP = KPP // 2
        N_LOAD = 4
        ADDED = NCH * PAIRS
        order = cst[:, C_ORDER:C_ORDER + E]

        def over_slots(ap):
            return ap.unsqueeze(1).broadcast_to([P, S72, E])

        def over_experts(ap):
            return ap.broadcast_to([P, S72, E])

        with nc.Block() as block:
            @block.sync
            def _(sp):
                def norm_pair(p):
                    sp.wait_ge(x2_ready, NCH * p + NCH)
                    sp.dma_start(x2_all[:, bass.ds(p, 1), :].rearrange("p o l -> p (o l)"), y2[:, :])\
                      .then_inc(x2_stored, 16)

                norm_pair(0)
                with nc.sync.Fori(1, PAIRS) as p:
                    norm_pair(p)
                sp.wait_ge(cw_copied, 3)
                for b in range(B):
                    sp.dma_start(cw_dram[:, L * b:L * b + IMG].rearrange("e (t j) -> t e j", t=KT), cw_t[:, b, :])\
                      .then_inc(cw_stored, 16)
                sp.dma_start(cw_dram.rearrange("e (b l) -> b e l", b=B)[:, :, IMG:L], cw_tail[:, :])\
                  .then_inc(cw_stored, 16)
                sp.wait_ge(cw_stored, 16 * (B + 1))
                sp.wait_ge(x2_stored, 16 * PAIRS)

                def load(n):
                    s = n % 2
                    sp.dma_start(x2[s][:, :], x2_all[:, n, :]).then_inc(loaded[s], 16)
                    sp.dma_start(h2[s][:, :], h2_all[:, n, :]).then_inc(loaded[s], 16)
                    for o in range(2):
                        src = cw_dram.rearrange("(k o) (n l) -> o n k l", o=2, n=PAIRS)[o, n]
                        sp.dma_start(cwb[s][D * o:D * o + D, :, :, :].rearrange("p k b l -> p k (b l)"),
                                     src.unsqueeze(0).broadcast_to([D, E // 2, 2 * L])).then_inc(loaded[s], 16)

                def store(n):
                    for bp in range(2):
                        b = 2 * n + bp
                        sp.wait_ge(gate_read, B + b + 1)
                        rows = out[b, 0:IMG, :].rearrange("(v t o) c -> o v t c", t=KT, o=2)
                        for o in range(2):
                            sp.dma_start(rows[o], outs[n % 2][bp][V * o:V * o + V, :, :]).then_inc(out_stored, 16)
                        sp.dma_start(out[b, IMG:L, :], out_tail[n % 2][bp][:, :]).then_inc(out_stored, 16)

                load(0)
                load(1)
                for n in range(PAIRS):
                    store(n)
                    sp.wait_ge(out_stored, 16 * 6 * (n + 1))
                    if n + 2 < PAIRS:
                        load(n + 2)

            @block.gpsimd
            def _(pool):
                def norm_pair(p):
                    for c in range(NCH):
                        pool.wait_ge(rstd2_dve, 2 * (NCH * p + c + 1))
                        if c == 0:
                            at_least(pool, x2_stored, 16 * p)
                            at_least(pool, gate_full, 2 * p)
                        nc.gpsimd.tensor_tensor(y2[:, chunk[c]], xc2[:, chunk[c]], rstd2[:, chunk[c]], ALU.mult)\
                          .then_inc(x2_ready, 1)

                norm_pair(0)
                with nc.gpsimd.Fori(1, PAIRS) as p:
                    norm_pair(p)
                def pair(n, s, r):
                    pool.wait_ge(loaded[s], 16 * N_LOAD * (r + 1))
                    for v in range(UPP):
                        bp, c = divmod(v, NCH)
                        dst = acc[:, bp, chunk[c]]
                        first = YPP * n + 4 * v
                        done = 4 * (UPP * n + v)
                        if v % NCH == 0:
                            pool.wait_ge(gate_full, B + 2 * n)
                        pool.wait_ge(x2_ready, ADDED + done)
                        pool.wait_ge(y_read, first + 2)
                        nc.gpsimd.tensor_tensor(dst, prod[:, 0, :], prod[:, 1, :], ALU.add).then_inc(x2_ready, 1)
                        for k in (2, 3):
                            pool.wait_ge(y_read, first + k + 1)
                            pool.wait_ge(x2_ready, ADDED + done + k - 1)
                            nc.gpsimd.tensor_tensor(dst, dst, prod[:, k, :], ALU.add).then_inc(x2_ready, 1)
                        pool.wait_ge(x2_ready, ADDED + done + 3)
                        rows = slice(D * bp, D * bp + D)
                        nc.gpsimd.tensor_tensor(acc[rows, bp, chunk[c]], acc[rows, bp, chunk[c]],
                                                h2[s][rows, chunk[c]], ALU.add).then_inc(x2_ready, 1)

                with nc.gpsimd.Fori(0, PAIRS // 2) as r:
                    for s in range(2):
                        pair(2 * r + s, s, r)

            @block.scalar
            def _(act):
                def norm_pair(p):
                    at_least(act, x2_ready, NCH * p)
                    for c in range(NCH):
                        act.wait_ge(centred, NCH * p + c + 1)
                        nc.scalar.activation(xc2[:, chunk[c]], banks[c][:, 0:CH], ACT.Copy)
                        nc.scalar.activation(sq2[:, chunk[c]], banks[c][:, 0:CH], ACT.Square).then_inc(sq_done, 1)
                    act.wait_ge(var_read, NCH * p + NCH)
                    guess_rstd(act, var2, rstd2, rstd2_sq, p, rstd2_act)

                norm_pair(0)
                with nc.scalar.Fori(1, PAIRS) as p:
                    norm_pair(p)
                act.wait_ge(gate_step, 2)
                nc.scalar.activation(gate_e[:, :, :], gate_e[:, :, :], ACT.Exp).then_inc(gate_exp, 1)

                with nc.scalar.Fori(0, PAIRS // 2) as r:
                    for s in range(2):
                        n = 2 * r + s
                        for v in range(UPP):
                            for e in range(E):
                                act.wait_ge(hid_full, KPP * n + E * v + e + 1)
                                if s > 0 or E * v + e >= 4:
                                    act.wait_ge(y_full, YPP * n + (E * v + e) // 2 - 1)
                                else:
                                    act.wait_ge(gate_full, B + 2 * n)
                                nc.scalar.activation(hid[:, e % 4, :], banks[e % 4][:, 0:CH], ACT.Gelu,
                                                     bias=b1_sb[:, e:e + 1]).then_inc(gelu_done, 1)
                            if v % NCH == NCH - 1:
                                bp = v // NCH
                                act.wait_ge(gate_full, B + 2 * n + bp + 1)
                                nc.scalar.activation(outs[s][bp][:, :, :].rearrange("p t c -> p (t c)"), banks[6][:, :],
                                                     ACT.Copy)
                                nc.scalar.activation(out_tail[s][bp][:, :], banks[7][0:TXT, 0:D], ACT.Copy)\
                                  .then_inc(gate_read, 1)

            @block.vector
            def _(dve):
                nc.vector.memset(logits[:, :, :], 0.0).then_inc(zeroed, 1)
                dve.wait_ge(zeroed, 1)
                def norm_pair(p):
                    for c in range(NCH):
                        dve.wait_ge(var_full, NCH * p + c + 1)
                        nc.vector.tensor_scalar(var2[:, chunk[c]], banks[3 + c][:, 0:CH], EPS, None, ALU.add)\
                          .then_inc(var_read, 1)
                    for c in range(NCH):
                        refine_rstd(dve, var2, rstd2, rstd2_sq, c, p, rstd2_act, rstd2_dve)
                    for bp in range(2):
                        dve.wait_ge(gate_full, 2 * p + bp + 1)
                        nc.vector.tensor_tensor(
                            logits[:, bass.ds(KT * (2 * p + bp), KT), :],
                            banks[6 + bp][:, 0:KT * E].rearrange("p (t e) -> p t e", e=E),
                            gate_bias[:, :].unsqueeze(1).broadcast_to([P, KT, E]), ALU.add)
                        nc.vector.tensor_tensor(
                            logits[0:TXT, bass.ds(KT * B + 2 * p + bp, 1), :].rearrange("p o e -> p (o e)"),
                            banks[6 + bp][0:TXT, KT * E:KT * E + E], gate_bias[0:TXT, :], ALU.add)\
                          .then_inc(gate_read, 1)

                norm_pair(0)
                with nc.vector.Fori(1, PAIRS) as p:
                    norm_pair(p)
                dve.wait_ge(gate_read, B)

                lg = logits[:, :, :]
                steps = [0]

                def step(ins):
                    ins.then_inc(gate_step, 1)
                    steps[0] += 1
                    dve.wait_ge(gate_step, steps[0])

                v = nc.vector
                step(v.tensor_reduce(top[:, :, :], lg, AX.X, ALU.max))
                step(v.tensor_tensor(gate_e[:, :, :], lg, over_experts(top[:, :, :]), ALU.subtract))
                step(v.tensor_tensor(hit[:, :, :], lg, over_experts(top[:, :, :]), ALU.is_equal))
                step(v.tensor_tensor(hit[:, :, :], hit[:, :, :], over_slots(order), ALU.mult))
                step(v.tensor_reduce(top[:, :, :], hit[:, :, :], AX.X, ALU.max))
                step(v.tensor_tensor(first_hot[:, :, :], hit[:, :, :], over_experts(top[:, :, :]), ALU.is_equal))
                step(v.scalar_tensor_tensor(out=rest[:, :, :], in0=first_hot[:, :, :], scalar=-3.0e38, in1=lg,
                                            op0=ALU.mult, op1=ALU.add))
                step(v.tensor_reduce(top[:, :, :], rest[:, :, :], AX.X, ALU.max))
                step(v.tensor_tensor(hit[:, :, :], rest[:, :, :], over_experts(top[:, :, :]), ALU.is_equal))
                step(v.tensor_tensor(hit[:, :, :], hit[:, :, :], over_slots(order), ALU.mult))
                step(v.tensor_reduce(top[:, :, :], hit[:, :, :], AX.X, ALU.max))
                step(v.tensor_tensor(hit[:, :, :], hit[:, :, :], over_experts(top[:, :, :]), ALU.is_equal))
                step(v.tensor_tensor(hit[:, :, :], hit[:, :, :], first_hot[:, :, :], ALU.add))
                dve.wait_ge(gate_exp, 1)
                step(v.tensor_reduce(total[:, :, :], gate_e[:, :, :], AX.X, ALU.add))
                step(v.reciprocal(total[:, :, :], total[:, :, :]))
                step(v.tensor_tensor(hit[:, :, :], hit[:, :, :], gate_e[:, :, :], ALU.mult))
                step(v.tensor_tensor(hit[:, :, :], hit[:, :, :], over_experts(total[:, :, :]), ALU.mult))
                dve.wait_ge(cw_full, 1)
                for k in range(2):
                    nc.vector.tensor_copy(cw_t[:, 4 * k:4 * k + 4, :].rearrange("p b j -> p (b j)"), banks[k][0:D, :])\
                      .then_inc(cw_copied, 1)
                nc.vector.tensor_copy(cw_tail[:, :], banks[2][0:D, 0:TXT]).then_inc(cw_copied, 1)

                with nc.vector.Fori(0, PAIRS // 2) as r:
                    for s in range(2):
                        n = 2 * r + s
                        dve.wait_ge(loaded[s], 16 * N_LOAD * (r + 1))
                        for v6 in range(UPP):
                            bp, c = divmod(v6, NCH)
                            for k in range(4):
                                dve.wait_ge(y_full, YPP * n + 4 * v6 + k + 1)
                                if s > 0 or v6 > 0:
                                    dve.wait_ge(x2_ready, ADDED + 4 * (UPP * n + v6 - 1) + max(k, 1))
                                else:
                                    dve.wait_ge(x2_ready, ADDED + 4 * UPP * n)
                                nc.vector.scalar_tensor_tensor(out=prod[:, k, :], in0=banks[4 + k % 2][:, 0:CH],
                                                               scalar=b2_sb[:, k:k + 1],
                                                               in1=cwb[s][:, k, bp, chunk[c]],
                                                               op0=ALU.add, op1=ALU.mult).then_inc(y_read, 1)

            @block.tensor
            def _(pe):
                def norm_pair(p):
                    at_least(pe, sq_done, NCH * p)
                    for c in range(NCH):
                        nc.tensor.matmul(banks[c][:, 0:CH], centre,
                                         h2_all[:, bass.ds(p, 1), chunk[c]].rearrange("p o l -> p (o l)"),
                                         start=True, stop=True).then_inc(centred, 1)
                    at_least(pe, var_read, NCH * p)
                    for c in range(NCH):
                        pe.wait_ge(sq_done, NCH * p + c + 1)
                        nc.tensor.matmul(banks[3 + c][:, 0:CH], mean, sq2[:, chunk[c]], start=True, stop=True)\
                          .then_inc(var_full, 1)
                    pe.wait_ge(x2_ready, NCH * p + NCH)
                    at_least(pe, gate_read, 2 * p)
                    for bp in range(2):
                        rows = slice(D * bp, D * bp + D)
                        for t in range(KT):
                            nc.tensor.matmul(banks[6 + bp][:, E * t:E * t + E], y2[rows, P * t:P * t + P],
                                             gate_sb[rows, :], start=True, stop=True)
                        nc.tensor.matmul(banks[6 + bp][0:TXT, E * KT:E * KT + E], y2[rows, IMG:L], gate_sb[rows, :],
                                         start=True, stop=True).then_inc(gate_full, 1)

                norm_pair(0)
                with nc.tensor.Fori(1, PAIRS) as p:
                    norm_pair(p)
                pe.wait_ge(gate_step, 17)
                for b in range(B):
                    nc.tensor.transpose(banks[b // 4][0:D, P * (b % 4):P * (b % 4) + P],
                                        hit[:, KT * b:KT * b + KT, :].rearrange("p t e -> p (t e)"), ident)
                nc.tensor.transpose(banks[2][0:D, 0:TXT], hit[0:TXT, KT * B:S72, :].rearrange("p t e -> p (t e)"),
                                    ident[0:TXT, 0:TXT])\
                  .then_inc(cw_full, 1)
                pe.wait_ge(cw_copied, 3)

                with nc.tensor.Fori(0, PAIRS // 2) as r:
                    for s in range(2):
                        n = 2 * r + s
                        pe.wait_ge(loaded[s], 16 * N_LOAD * (r + 1))

                        def experts_out(v, k):
                            pe.wait_ge(gelu_done, KPP * n + E * v + 2 * k + 2)
                            if s > 0 or 4 * v + k >= 2:
                                pe.wait_ge(y_read, YPP * n + 4 * v + k - 1)
                            for o in range(2):
                                e = 2 * k + o
                                last = nc.tensor.matmul(banks[4 + k % 2][D * o:D * o + D, 0:CH], w2_sb[:, e, :],
                                                        hid[:, e % 4, :], start=True, stop=True)
                            last.then_inc(y_full, 1)

                        for v in range(UPP):
                            bp, c = divmod(v, NCH)
                            rows = slice(D * bp, D * bp + D)
                            for k in range(4):
                                for e in (2 * k, 2 * k + 1):
                                    if s > 0 or E * v + e >= 4:
                                        pe.wait_ge(gelu_done, KPP * n + E * v + e - 3)
                                    nc.tensor.matmul(banks[e % 4][:, 0:CH], w1_sb[rows, e, :], x2[s][rows, chunk[c]],
                                                     start=True, stop=True).then_inc(hid_full, 1)
                                if k > 0:
                                    experts_out(v, k - 1)
                            experts_out(v, 3)
                            if c == NCH - 1:
                                pe.wait_ge(x2_ready, ADDED + 4 * (UPP * n + v + 1))
                                pe.wait_ge(gate_read, B + 2 * n + bp)
                                for t in range(KT):
                                    nc.tensor.matmul(banks[6][:, D * t:D * t + D], acc[:, bp, P * t:P * t + P], fold,
                                                     start=True, stop=True)
                                nc.tensor.matmul(banks[7][0:TXT, 0:D], acc[:, bp, IMG:L], fold,
                                                 start=True, stop=True).then_inc(gate_full, 1)


def constants():
    import numpy as np

    c = np.zeros((P, C_COLS), np.float32)
    i = np.arange(P)
    same = (i[:, None] // D == i[None, :] // D) / D
    c[:, C_ID:C_ID + P] = np.eye(P)
    c[:, C_CENTRE:C_CENTRE + P] = np.eye(P) - same
    c[:, C_MEAN:C_MEAN + P] = same
    c[:, C_TAIL:C_TAIL + TXT] = i[:, None] % 32 == np.arange(TXT)[None, :]
    c[:, C_DEN:C_DEN + P] = (i[:, None] // 32 == i[None, :] // 32) & (i[:, None] % 32 == DH)
    c[:, C_FOLD:C_FOLD + D] = i[:, None] % D == np.arange(D)[None, :]
    t = np.arange(PATCH).reshape(2, 2, 4).transpose(1, 0, 2).reshape(PATCH)
    angle = 2 * np.pi * np.arange(NFREQ)[:, None] * t[None, :] / PATCH
    c[0:NFREQ, C_DFT:C_DFT + PATCH] = np.cos(angle) / np.sqrt(PATCH)
    c[NFREQ:2 * NFREQ, C_DFT:C_DFT + PATCH] = -np.sin(angle) / np.sqrt(PATCH)
    c[:, C_ORDER:C_ORDER + E] = E - np.arange(E)
    return c


_INS = ["x", "txt", "L0_tok_W", "L0_attn_w_qkv", "L0_attn_w_proj", "L0_attn_b_proj", "L0_ffn_gate_w",
        "L0_ffn_gate_b", "L0_ffn_W1", "L0_ffn_b1", "L0_ffn_W2", "L0_ffn_b2"]


def kernel(**inputs):
    import numpy as np
    import concourse.bacc as bacc
    from concourse.bass_utils import run_bass_kernel_spmd

    nc = bacc.Bacc("TRN2", target_bir_lowering=False, num_devices=1)
    arrays = {f"in_{name}": np.ascontiguousarray(inputs[name]) for name in _INS}
    arrays["in_constants"] = constants()
    args = [nc.dram_tensor(n, a.shape, mybir.dt.from_np(a.dtype), kind="ExternalInput").ap() for n, a in arrays.items()]
    out = nc.dram_tensor("out_0", (B, L, D), F32, kind="ExternalOutput").ap()
    build(nc, *args, out)
    return run_bass_kernel_spmd(nc, [arrays], core_ids=[0]).results[0]["out_0"]
```

```python
from contextlib import ExitStack

import concourse.bass as bass
from concourse import mybir

F32 = mybir.dt.float32
BF16 = mybir.dt.bfloat16
I32 = mybir.dt.int32
ALU = mybir.AluOpType
ACT = mybir.ActivationFunctionType
AX = mybir.AxisListType

P = 128
B, C, T, V = 8, 64, 128, 64
TXT = 32
D = 64
PATCH, STRIDE = 16, 8
NPATCH = T // STRIDE
NFREQ = PATCH // 2 + 1
IMG = V * NPATCH
L = IMG + TXT
H, DH = 4, 16
E, HID = 8, 128
PAIRS = B // 2
CH = L // 3
NCH = 3
QTP = IMG // P + 1
LP = QTP * P
KT = IMG // P
HALF = IMG // 2
SCALE = float(DH) ** -0.5
EPS = 1e-5
ROWS = 6 * DH
UNITS = NCH * (1 + KT * H)
GROUPS = NCH * KT
QT = H * KT
MAXU = 2 * QT + 2 + NCH
PARTS = [(0, 0), (0, 1), (1, 0), (0, 2), (1, 1), (2, 0)]

C_ID, C_CENTRE, C_MEAN, C_DEN, C_FOLD, C_DFT, C_ORDER, C_TAIL = 0, 128, 256, 384, 512, 576, 592, 600
C_COLS = 632

AT_VALUES = [0, 3]
AT_RECIP = 5
AT_FINISH = [15, 18, 21, 24, 27, 30]
AT_EMBED = [list(range(32, 47, 2)), list(range(48, 63, 2))]
AT_TOKENISE = [AT_EMBED[0][-1], AT_EMBED[1][-1], 65, 68, 71, 74, 77, 80, 82, 84]
FIRST_MAX = 14
AT_SHIFT = FIRST_MAX + 72
AT_PROJECT = {"odd": [34, 37, 40], "even": [89, 92, 95]}
EARLY_PROJECT = [4, 7, 10]
EARLY_VALUES = [13, 16]
EARLY_EMBED = [list(range(20, 35, 2)), list(range(36, 51, 2))]
EARLY_TOKENISE = [EARLY_EMBED[0][-1], EARLY_EMBED[1][-1], 51, 52, 54, 56, 58, 61, 63, 65]
PV_LAG = 2 * H

N_SETUP = 11
SHIFT_DMAS = 3
N_FFN = 8
PRESETS = 21

USES = {"tokenise": 10, "project": 3, "values": 2, "shift": 1, "finish": 6}


def build(nc, x, txt, tok_w, w_qkv, w_proj, b_proj, gate_w, gate_b, w1, b1, w2, b2, consts, out):
    with ExitStack() as ctx:
        def sb(name, shape, dt=F32):
            return ctx.enter_context(nc.sbuf_tensor(name, shape, dt))

        def bank(name):
            return ctx.enter_context(nc.psum_tensor(name, [P, 512], F32))

        def sem(name):
            return ctx.enter_context(nc.semaphore(name))

        cw_dram = nc.dram_tensor("gates_by_expert", [E, B * L], F32, kind="Internal").ap()

        cst = sb("cst", [P, C_COLS])
        ident = cst[:, C_ID:C_ID + P]
        centre = cst[:, C_CENTRE:C_CENTRE + P]
        mean = cst[:, C_MEAN:C_MEAN + P]
        den_sel = cst[:, C_DEN:C_DEN + P]
        fold = cst[:, C_FOLD:C_FOLD + D]
        qkv_in = sb("qkv_in", [P, 2, D])
        v_in = sb("v_in", [D, 2, D])
        proj_in = sb("proj_in", [D, H, 32])
        qkT = sb("qkT", [P, P])
        vT = sb("vT", [P, 2, D])
        projT = sb("projT", [P, D])
        proj_bias = sb("proj_bias", [P, 1])
        gate_sb = sb("gate_sb", [P, E])
        gate_bias = sb("gate_bias", [P, E])
        w1_sb = sb("w1_sb", [P, E, HID])
        w01, w10, w20 = [sb(name, [P, E, HID], BF16) for name in ("w01", "w10", "w20")]
        w2_sb = sb("w2_sb", [P, E, D])
        biases = sb("biases", [P, E + E // 2])
        b1_sb, b2_sb = biases[:, 0:E], biases[:, E:E + E // 2]
        bias_in = sb("bias_in", [E + E // 2, P])
        tok_m = sb("tok_m", [P, 8, D])
        h2_all = sb("h2_all", [P, PAIRS, L])
        h_res = sb("h_res", [P, L])

        xc = sb("xc", [P, L])
        sq = sb("sq", [P, L])
        xn = sb("xn", [P, L])
        roots = sb("roots", [P, 2 * KT + 2])
        root_work = sb("root_work", [P, 2, 2 * KT + 2])
        qk_part = x_part = [sb(f"part{i}", [P, L], BF16) for i in range(3)]
        x_rest = sq
        TILES = 2 * KT + 2
        gate_pair = sb("gate_pair", [P, 2, E])
        logits = sb("logits", [P, TILES, E])
        gate_e = sb("gate_e", [P, TILES, E])
        rest = sb("rest", [P, TILES, E])
        hit = sb("hit", [P, TILES, E])
        first_hot = sb("first_hot", [P, TILES, E])
        top = sb("top", [P, TILES, 1])
        total = sb("total", [P, TILES, 1])
        cw_t = sb("cw_t", [P, P])
        cw_tail = sb("cw_tail", [2 * E, TXT])

        banks = [bank(f"bank{i}") for i in range(8)]
        score_bank = banks[0:3]
        o_bank = banks[3]
        max_bank = banks[4:7]
        side_bank = banks[7]

        setup_loaded = sem("setup_loaded")
        ffn_loaded = sem("ffn_loaded")
        preset = sem("preset")
        setup_psum = sem("setup_psum")
        setup_done = sem("setup_done")
        x_loaded = sem("x_loaded")
        side_full = sem("side_full")
        side_free = sem("side_free")
        roots_step = sem("roots_step")
        roots2_step = sem("roots2_step")
        h_copied = sem("h_copied")
        h_stored = sem("h_stored")
        part1_done = sem("part1_done")
        part2_done = sem("part2_done")
        part3_done = sem("part3_done")
        w_split = sem("w_split")
        stacked = sem("stacked")
        v_ready = sem("v_ready")
        max_scores = sem("max_scores")
        max_done = sem("max_done")
        neg_max = sem("neg_max")
        shift_step = sem("shift_step")
        shifted = sem("shifted")
        scores_ready = sem("scores_ready")
        exp_done = sem("exp_done")
        pv_done = sem("pv_done")
        o_ready = sem("o_ready")
        o_free = sem("o_free")
        den_moved = sem("den_moved")
        recip_done = sem("recip_done")
        recip_moved = sem("recip_moved")
        on_ready = sem("on_ready")

        norm_full = sem("norm_full")
        norm_read = sem("norm_read")
        x_part0 = sem("x_part0")
        x_split = sem("x_split")
        x_stacked = [sem("x_stacked0"), sem("x_stacked1")]
        gate_step = sem("gate_step")
        gate_exp = sem("gate_exp")
        cw_stored = sem("cw_stored")
        cw_loaded = [sem("cw_loaded0"), sem("cw_loaded1")]
        h2_loaded = [sem("h2_loaded0"), sem("h2_loaded1")]
        hid_full = sem("hid_full")
        gelu_done = sem("gelu_done")
        y_full = sem("y_full")
        y_read = sem("y_read")
        summed = sem("summed")
        out_full = sem("out_full")
        out_read = sem("out_read")
        out_stored = sem("out_stored")
        zeroed = sem("zeroed")

        phase1 = ExitStack()

        def sb1(name, shape, dt=F32):
            return phase1.enter_context(nc.sbuf_tensor(name, shape, dt))

        xt = [sb1(f"x{i}", [P, NPATCH + 1, 4, V]) for i in range(2)]
        text_in = sb1("text_in", [TXT, 2, D])
        h_new = sb1("h_new", [P, L])
        qk_rest = sb1("qk_rest", [P, L])
        qs = [sb1(f"q_stack{i}", [P, H, LP], BF16) for i in range(2)]
        ks = [sb1(f"k_stack{i}", [P, H, LP], BF16) for i in range(2)]
        v_tiles = [sb1(f"v_tiles{i}", [P, KT, H, 32]) for i in range(2)]
        v_tail = [sb1(f"v_tail{i}", [P, P]) for i in range(2)]
        max_parts = sb1("max_parts", [P, QT, 3])
        max_tail = sb1("max_tail", [P, NCH])
        negm = sb1("negm", [P, 2, P])
        m_part = sb1("m_part", [H * QTP, 3, P], BF16)
        m_rest = sb1("m_rest", [H * QTP, P])
        probs = sb1("probs", [P, 3, H, CH])
        tok_in = probs[0:2 * NFREQ, :, :, :].rearrange("r i h l -> r (i h l)")[:, 0:D * C]\
            .rearrange("r (d c) -> r d c", c=C)
        probs_tail = [sb1(f"probs_tail{i}", [P, CH]) for i in range(NCH)]
        ot = [sb1(f"heads_out{i}", [P, L]) for i in range(2)]
        den = sb1("den", [P, H * L // P])
        recip_rows = sb1("recip_rows", [P, L])
        recip = sb1("recip", [P, L])
        on = sb1("on", [P, L])

        g_values0 = USES["tokenise"] + USES["project"]
        g_project1 = g_values0 + USES["values"]
        g_values1 = g_project1 + USES["project"]
        g_tokenise1 = g_values1 + USES["values"]
        g_shift0 = g_tokenise1 + USES["tokenise"]
        g_slot0 = g_shift0 + 1
        per_slot = USES["values"] + USES["finish"] + USES["shift"] + USES["project"]
        g_slot1 = g_slot0 + USES["shift"] + USES["project"]
        per_round = 2 * per_slot + USES["tokenise"]
        g_epilogue = g_slot1 + 2 * per_round + 2 * per_slot - USES["project"] + USES["finish"]

        def slot_plan(odd, q):
            return (2 * q + 1, g_slot1 + per_round * q) if odd else (2 * q + 2, g_slot1 + per_slot + per_round * q)

        def side_steps(u, stages, b, par, q, g):
            ahead = q + 1 if par else q + 2
            order = []
            if u == 0:
                for i in range(2):
                    if "maxima" in stages:
                        order.append(("stack", i, b + 1, 1 - par, q + 1, g))
                    if "finish" in stages:
                        order.append(("spread", i, b - 1, 1 - par, q, g))
            if u == AT_RECIP and "finish" in stages:
                order.append(("recip", 0, b - 1, 1 - par, q, g))
            if u == 0 and "load" in stages:
                order.append(("load", 0, None, None, q + 2, g))
            for stage, at, t, tpar, pair in (("values", AT_VALUES, b + 1, 1 - par, q + 1),
                                             ("finish", AT_FINISH, b - 1, 1 - par, q),
                                             ("tokenise", AT_TOKENISE, None, None, q + 2),
                                             ("project", AT_PROJECT["odd"] if par else [], b + 2, par, ahead),
                                             ("shift", [AT_SHIFT], b + 1, 1 - par, q + 1),
                                             ("project", [] if par else AT_PROJECT["even"], b + 2, par, ahead)):
                if stage in stages:
                    if u in at:
                        order.append((stage, at.index(u), t, tpar, pair, g))
                    if stage == "tokenise":
                        for i in range(2):
                            if u in AT_EMBED[i][:-1]:
                                order.append(("embed", (i, AT_EMBED[i].index(u)), None, None, pair, g))
                    if at:
                        g = g + USES[stage]
            if "maxima" in stages and FIRST_MAX <= u < FIRST_MAX + MAXU:
                order.append(("maxima", u - FIRST_MAX, b + 1, 1 - par, q + 1, g))
            return order

        FIRST_NORM = {10: [("centre", 0)], 12: [("centre", 1)], 14: [("centre", 2)], 18: [("roots", 0)],
                      22: [("scale", 0)], 24: [("scale", 1)], 26: [("scale", 2)], 29: [("gates", 0)],
                      32: [("split", 0), ("choose", 0)], 35: [("split", 1), ("choose", 1)],
                      38: [("split", 2), ("choose", 2)], 41: [("choose", 3)], 44: [("choose", 4)],
                      47: [("choose", 5)], 52: [("turn", 0)]}

        NEXT = ("values", "maxima", "shift")
        BESIDE = {0: ("maxima", "shift", "project"), "odd": NEXT + ("load", "project", "finish"),
                  "even": NEXT + ("project", "finish", "tokenise"), 5: NEXT + ("project", "finish"),
                  6: NEXT + ("finish",), 7: ("finish",)}

        def run_phase1(eng, attend_unit, side, after_slot, norm_step=None):
            def slot(b, par, q, g, stages):
                for u in range(UNITS):
                    attend_unit(b, par, u, g)
                    for step in side_steps(u, stages, b, par, q, g):
                        side(*step)
                    if isinstance(b, int) and b == B - 1 and norm_step:
                        for name, i in FIRST_NORM.get(u, []):
                            norm_step(eng, name, i, 0)
                after_slot(b, par)

            for i in range(USES["tokenise"]):
                for j in range(7 if i < 2 else 0):
                    side("embed", (i, j), None, None, 0, 0)
                side("tokenise", i, None, None, 0, 0)
            for i in range(USES["project"]):
                side("project", i, 0, 0, 0, USES["tokenise"])
            for i in range(2):
                side("stack", i, 0, 0, 0, 0)
            for i in range(USES["values"]):
                side("values", i, 0, 0, 0, g_values0)
            for u in range(MAXU):
                side("maxima", u, 0, 0, 0, g_project1)
                if u in EARLY_PROJECT:
                    side("project", EARLY_PROJECT.index(u), 1, 1, 0, g_project1)
                if u in EARLY_VALUES:
                    side("values", EARLY_VALUES.index(u), 1, 1, 0, g_values1)
                for i, at in enumerate(EARLY_TOKENISE):
                    if i < 2 and u in EARLY_EMBED[i][:-1]:
                        side("embed", (i, EARLY_EMBED[i].index(u)), None, None, 1, g_tokenise1)
                    if u == at:
                        side("tokenise", i, None, None, 1, g_tokenise1)
            side("shift", 0, 0, 0, 0, g_shift0)
            slot(0, 0, -1, g_slot0, BESIDE[0])
            with eng.Fori(0, 2) as q:
                b, g = slot_plan(True, q)
                slot(b, 1, q, g, BESIDE["odd"])
                b, g = slot_plan(False, q)
                slot(b, 0, q, g, BESIDE["even"])
            b, g = slot_plan(True, 2)
            slot(b, 1, 2, g, BESIDE[5])
            slot(6, 0, 2, g + per_slot, BESIDE[6])
            g7 = g + 2 * per_slot - USES["project"]
            slot(7, 1, 3, g7, BESIDE[7])
            for stage, i in (("spread", 0), ("recip", 0), ("spread", 1)):
                side(stage, i, 7, 1, 3, g7)
            for i in range(USES["finish"]):
                side("finish", i, 7, 1, 3, g_epilogue)
            assert g_epilogue == g7 + USES["finish"]

        def at_least(eng, s, value):
            if not isinstance(value, int) or value > 0:
                eng.wait_ge(s, value)

        def in_prologue(g):
            return isinstance(g, int) and g < g_values0

        def in_epilogue(g):
            return isinstance(g, int) and g == g_epilogue

        def step_bank(i, g):
            return banks[(g + i) % 8] if in_prologue(g) else banks[i] if in_epilogue(g) else side_bank

        def all_free(i, g):
            return in_prologue(g) and g + i in (1, 2, 4, 5, 8, 9, 11, 12) or in_epilogue(g) and i in (2, 4)

        def full(eng, i, g):
            eng.wait_ge(side_full, g + i + 1)
            return step_bank(i, g)

        def freed(eng, i, g):
            at_least(eng, side_free, g + i + 1)

        X_DMAS = 9
        ROOT_STEPS = 12
        chunk = [slice(c * CH, (c + 1) * CH) for c in range(NCH)]

        NORM_TILES = [slice(P * t, min(P * t + P, L)) for t in range(KT + 1)]
        WIDE = 3 * P
        wide = [slice(WIDE * i, min(WIDE * i + WIDE, L)) for i in range(NCH)]

        def token_variances(bank, squares):
            for t, tokens in enumerate(NORM_TILES):
                rows = slice(0, tokens.stop - tokens.start)
                last = nc.tensor.matmul(bank[rows, 2 * t:2 * t + 2], squares[:, tokens], mean[:, 0:P:D],
                                        start=True, stop=True)
            return last

        def inverse_roots(dve, y, work, bank, done, n):
            v, t = work[:, 0, :], work[:, 1, :]
            base = ROOT_STEPS * n
            full, tail = slice(0, 2 * KT), slice(2 * KT, 2 * KT + 2)
            nc.vector.tensor_scalar(v[:, full], bank[:, full], EPS, None, ALU.add).then_inc(done, 1)
            nc.vector.tensor_scalar(v[0:TXT, tail], bank[0:TXT, tail], EPS, None, ALU.add).then_inc(done, 1)
            dve.wait_ge(done, base + 2)
            nc.vector.tensor_scalar(t.bitcast(I32), v.bitcast(I32), 1, None, ALU.arith_shift_right).then_inc(done, 1)
            dve.wait_ge(done, base + 3)
            nc.vector.tensor_scalar(y.bitcast(I32), t.bitcast(I32), -1, 0x5F3759DF, ALU.mult, ALU.add).then_inc(done, 1)
            step = base + 4
            for newton in range(3):
                dve.wait_ge(done, step)
                nc.vector.tensor_tensor(t, y, y, ALU.mult).then_inc(done, 1)
                dve.wait_ge(done, step + 1)
                nc.vector.scalar_tensor_tensor(out=t, in0=v, scalar=-0.5, in1=t, op0=ALU.mult, op1=ALU.mult)\
                  .then_inc(done, 1)
                dve.wait_ge(done, step + 2)
                last = nc.vector.scalar_tensor_tensor(out=y, in0=t, scalar=1.5, in1=y, op0=ALU.add, op1=ALU.mult)
                if newton < 2:
                    last.then_inc(done, 1)
                step += 3
            return last

        def spread_roots(bank, roots, i):
            for t in range(3 * i, 3 * i + 3):
                tokens = NORM_TILES[t]
                n = tokens.stop - tokens.start
                for bp in range(2):
                    last = nc.tensor.matmul(bank[D * bp:D * bp + D, tokens.start - WIDE * i:tokens.stop - WIDE * i],
                                            roots[0:n, 2 * t + bp:2 * t + bp + 1].broadcast_to([n, D]),
                                            ident[0:n, 0:n], start=True, stop=True)
            return last

        X_STACKS = 4
        KPB = NCH * E
        YPB = KPB // 2
        NORM_FILLS = 2 * NCH + 3
        ROOTS, GATES, TURN = NCH, 2 * NCH + 1, 2 * NCH + 2
        CHOICE = 17
        order = cst[:, C_ORDER:C_ORDER + E]

        def norm_bank(p, fill):
            return banks[4 + fill % 3] if isinstance(p, int) and p == 0 else banks[7]

        def over_slots(ap):
            return ap.unsqueeze(1).broadcast_to([P, TILES, E])

        def over_experts(ap):
            return ap.broadcast_to([P, TILES, E])

        def norm_scalar(act, name, i, p):
            if name == "centre":
                if i == 0:
                    at_least(act, x_split, 3 * p)
                act.wait_ge(norm_full, NORM_FILLS * p + i + 1)
                src = norm_bank(p, i)[:, 0:CH]
                nc.scalar.activation(xc[:, chunk[i]], src, ACT.Copy)
                nc.scalar.activation(sq[:, chunk[i]], src, ACT.Square).then_inc(norm_read, 1)
            elif name == "gates":
                act.wait_ge(norm_read, NORM_FILLS * p + GATES)
                for stacks in x_stacked:
                    at_least(act, stacks, 16 * X_STACKS * p)
                nc.scalar.activation(x_part[0][:, :], xn[:, :], ACT.Copy).then_inc(x_part0, 1)
            elif (name, i) == ("choose", 1):
                act.wait_ge(gate_step, CHOICE * p + 2)
                nc.scalar.activation(gate_e[:, :, :], gate_e[:, :, :], ACT.Exp).then_inc(gate_exp, 1)

        v = nc.vector
        lg = logits[:, :, :]
        CHOOSE = [
            lambda: v.tensor_reduce(top[:, :, :], lg, AX.X, ALU.max),
            lambda: v.tensor_tensor(gate_e[:, :, :], lg, over_experts(top[:, :, :]), ALU.subtract),
            lambda: v.tensor_tensor(hit[:, :, :], lg, over_experts(top[:, :, :]), ALU.is_equal),
            lambda: v.tensor_tensor(hit[:, :, :], hit[:, :, :], over_slots(order), ALU.mult),
            lambda: v.tensor_reduce(top[:, :, :], hit[:, :, :], AX.X, ALU.max),
            lambda: v.tensor_tensor(first_hot[:, :, :], hit[:, :, :], over_experts(top[:, :, :]), ALU.is_equal),
            lambda: v.scalar_tensor_tensor(out=rest[:, :, :], in0=first_hot[:, :, :], scalar=-3.0e38, in1=lg,
                                           op0=ALU.mult, op1=ALU.add),
            lambda: v.tensor_reduce(top[:, :, :], rest[:, :, :], AX.X, ALU.max),
            lambda: v.tensor_tensor(hit[:, :, :], rest[:, :, :], over_experts(top[:, :, :]), ALU.is_equal),
            lambda: v.tensor_tensor(hit[:, :, :], hit[:, :, :], over_slots(order), ALU.mult),
            lambda: v.tensor_reduce(top[:, :, :], hit[:, :, :], AX.X, ALU.max),
            lambda: v.tensor_tensor(hit[:, :, :], hit[:, :, :], over_experts(top[:, :, :]), ALU.is_equal),
            lambda: v.tensor_tensor(hit[:, :, :], hit[:, :, :], first_hot[:, :, :], ALU.add),
            lambda: v.tensor_reduce(total[:, :, :], gate_e[:, :, :], AX.X, ALU.add),
            lambda: v.reciprocal(total[:, :, :], total[:, :, :]),
            lambda: v.tensor_tensor(hit[:, :, :], hit[:, :, :], gate_e[:, :, :], ALU.mult),
            lambda: v.tensor_tensor(hit[:, :, :], hit[:, :, :], over_experts(total[:, :, :]), ALU.mult),
        ]

        def norm_vector(dve, name, i, p):
            if name == "centre" and isinstance(p, int) and p == 0:
                if i == 0:
                    dve.wait_ge(ffn_loaded, 16 * N_FFN)
                    v.memset(logits[:, :, :], 0.0).then_inc(zeroed, 1)
                    v.memset(gate_pair[:, :, :], 0.0).then_inc(zeroed, 1)
                    dve.wait_ge(zeroed, 2)
                    for bp in range(2):
                        rows = slice(D * bp, D * bp + D)
                        v.tensor_copy(gate_pair[rows, bp, :], gate_sb[rows, :]).then_inc(zeroed, 1)
            elif name == "roots":
                dve.wait_ge(norm_full, NORM_FILLS * p + ROOTS + 1)
                inverse_roots(dve, roots[:, :], root_work, norm_bank(p, ROOTS), roots2_step, p).then_inc(norm_read, 1)
            elif name == "scale":
                fill, tokens = ROOTS + 1 + i, wide[i]
                dve.wait_ge(norm_full, NORM_FILLS * p + fill + 1)
                v.tensor_tensor(xn[:, tokens], xc[:, tokens],
                                norm_bank(p, fill)[:, 0:tokens.stop - tokens.start], ALU.mult)\
                  .then_inc(norm_read, 1)
            elif name == "gates":
                dve.wait_ge(norm_full, NORM_FILLS * p + GATES + 1)
                bank = norm_bank(p, GATES)
                for bp in range(2):
                    v.tensor_tensor(logits[:, KT * bp:KT * bp + KT, :],
                                    bank[:, 0:P].rearrange("p (t b e) -> p b t e", b=2, e=E)[:, bp],
                                    gate_bias[:, :].unsqueeze(1).broadcast_to([P, KT, E]), ALU.add)
                v.tensor_tensor(logits[0:TXT, 2 * KT:TILES, :],
                                bank[0:TXT, P:P + 2 * E].rearrange("p (b e) -> p b e", e=E),
                                gate_bias[0:TXT, :].unsqueeze(1).broadcast_to([TXT, 2, E]), ALU.add)\
                  .then_inc(norm_read, 1)
            elif name == "choose":
                if i == 0:
                    dve.wait_ge(norm_read, NORM_FILLS * p + GATES + 1)
                for j in range(3 * i, min(3 * i + 3, CHOICE)):
                    if j > 0:
                        dve.wait_ge(gate_step, CHOICE * p + j)
                    if j == 13:
                        dve.wait_ge(gate_exp, p + 1)
                    CHOOSE[j]().then_inc(gate_step, 1)
            elif name == "split":
                if i == 0:
                    dve.wait_ge(x_part0, p + 1)
                    ins = v.tensor_tensor(x_rest[:, :], xn[:, :], x_part[0][:, :], ALU.subtract)
                elif i == 1:
                    dve.wait_ge(x_split, 3 * p + 1)
                    ins = v.tensor_copy(x_part[1][:, :], x_rest[:, :])
                else:
                    dve.wait_ge(x_split, 3 * p + 2)
                    ins = v.tensor_tensor(x_part[2][:, :], x_rest[:, :], x_part[1][:, :], ALU.subtract)
                ins.then_inc(x_split, 1)
            elif name == "turn":
                dve.wait_ge(norm_full, NORM_FILLS * p + TURN + 1)
                at_least(dve, cw_stored, 16 * 3 * p)
                bank = norm_bank(p, TURN)
                v.tensor_copy(cw_t[:, :], bank[:, 0:P])
                v.tensor_copy(cw_tail[:, :], bank[0:2 * E, P:P + TXT]).then_inc(norm_read, 1)

        def norm_tensor(pe, name, i, p):
            fill = {"centre": i, "roots": ROOTS, "scale": ROOTS + 1 + i, "gates": GATES, "turn": TURN}.get(name)
            if fill is None:
                return
            bank = norm_bank(p, fill)
            if not (isinstance(p, int) and p == 0 and name in ("centre", "scale") and i > 0):
                at_least(pe, norm_read, NORM_FILLS * p + fill)
            if name == "centre":
                if i == 0:
                    pe.wait_ge(h_stored, 16 * (p + 1))
                    at_least(pe, out_read, 2 * p - 3)
                last = nc.tensor.matmul(bank[:, 0:CH], centre,
                                        h2_all[:, bass.ds(p, 1), chunk[i]].rearrange("p o l -> p (o l)"),
                                        start=True, stop=True)
            elif name == "roots":
                last = token_variances(bank, sq)
            elif name == "scale":
                last = spread_roots(bank, roots, i)
            elif name == "gates":
                pe.wait_ge(zeroed, 4)
                at_least(pe, out_read, 2 * p - 2)
                for t in range(KT):
                    nc.tensor.matmul(bank[:, 2 * E * t:2 * E * t + 2 * E], xn[:, P * t:P * t + P],
                                     gate_pair[:, :, :].rearrange("p b e -> p (b e)"), start=True, stop=True)
                last = nc.tensor.matmul(bank[0:TXT, P:P + 2 * E], xn[:, IMG:L],
                                        gate_pair[:, :, :].rearrange("p b e -> p (b e)"), start=True, stop=True)
            else:
                pe.wait_ge(gate_step, CHOICE * (p + 1))
                nc.tensor.transpose(bank[:, 0:P], hit[:, 0:2 * KT, :].rearrange("p t e -> p (t e)"), ident)
                last = nc.tensor.transpose(bank[0:2 * E, P:P + TXT],
                                           hit[0:TXT, 2 * KT:TILES, :].rearrange("p t e -> p (t e)"),
                                           ident[0:TXT, 0:TXT])
            last.then_inc(norm_full, 1)

        def store_gates(sp, p):
            sp.wait_ge(norm_read, NORM_FILLS * (p + 1))
            for bp in range(2):
                first = L * (2 * p + bp)
                sp.dma_start(cw_dram[:, first:first + IMG].rearrange("e (t j) -> t e j", t=KT),
                             cw_t[D * bp:D * bp + D, :]).then_inc(cw_stored, 16)
            sp.dma_start(cw_dram.rearrange("e (b l) -> b e l", b=B)[2 * p:2 * p + 2, :, IMG:L], cw_tail[:, :])\
              .then_inc(cw_stored, 16)
            sp.wait_ge(cw_stored, 16 * 3 * (p + 1))


        with nc.Block() as block:

            @block.sync
            def _(sp):
                def load_x(pair):
                    for bp in range(2):
                        src = x[bass.ds(2 * pair + bp, 1)].rearrange("o c t v -> (o c) t v")
                        for th in range(2):
                            part = slice(C * th, C * th + C)
                            sp.dma_start(xt[bp][part, 0:NPATCH, :, :],
                                         src.rearrange("c (j h t) v -> h c j t v", h=2, t=4)[th])\
                              .then_inc(x_loaded, 16)
                            sp.dma_start(xt[bp][part, NPATCH, :, :],
                                         src[:, T - 1:T, :].broadcast_to([C, 4, V])).then_inc(x_loaded, 16)
                    sp.dma_start(text_in[:, :, :], txt[bass.ds(2 * pair, 2)].rearrange("b t d -> t b d"))\
                      .then_inc(x_loaded, 16)

                sp.dma_start(cst[:, :], consts).then_inc(setup_loaded, 16)
                sp.dma_start(tok_in[:, :, :], tok_w.rearrange("d (r c) -> r d c", c=C)).then_inc(setup_loaded, 16)
                for s in range(2):
                    for half in range(2):
                        sp.dma_start(qkv_in[D * s:D * s + D, half, :],
                                     w_qkv[D * s:D * s + D, :].rearrange("(h d) c -> d h c", h=H))\
                          .then_inc(setup_loaded, 16)
                for half in range(2):
                    sp.dma_start(v_in[:, half, :], w_qkv[2 * D:3 * D, :]).then_inc(setup_loaded, 16)
                sp.dma_start(bias_in[0:E, :], b1).then_inc(setup_loaded, 16)
                sp.dma_start(bias_in[E:E + E // 2, :], b2.rearrange("(k o) n -> k (o n)", o=2))\
                  .then_inc(setup_loaded, 16)
                sp.wait_ge(preset, 1)
                sp.dma_start(proj_in[:, :, 0:DH], w_proj.rearrange("n (h d) -> n h d", h=H)).then_inc(setup_loaded, 16)
                load_x(0)
                for half in range(2):
                    rows = slice(D * half, D * half + D)
                    sp.dma_start(proj_bias[rows, :], b_proj.rearrange("(n o) -> n o", o=1)).then_inc(ffn_loaded, 16)
                    sp.dma_start(gate_sb[rows, :], gate_w).then_inc(ffn_loaded, 16)
                    sp.dma_start(w1_sb[rows, :, :], w1.rearrange("e c n -> c e n")).then_inc(ffn_loaded, 16)
                sp.dma_start(gate_bias[:, :], gate_b.rearrange("(o e) -> o e", o=1).broadcast_to([P, E]))\
                  .then_inc(ffn_loaded, 16)
                sp.dma_start(w2_sb[:, :, :], w2.rearrange("e n c -> n e c")).then_inc(ffn_loaded, 16)

                def stack_parts(par, products):
                    for n in products:
                        a, k = PARTS[n]
                        rows = slice(DH * n, DH * n + DH)
                        sp.dma_start(qs[par][rows, :, 0:L], qk_part[a][0:D, :]).then_inc(stacked, 16)
                        sp.dma_start(ks[par][rows, :, 0:L], qk_part[k][D:P, :]).then_inc(stacked, 16)

                def attend_unit(b, par, u, g):
                    pass

                def side(stage, i, t, par, pair, g):
                    if (stage, i) == ("spread", 0):
                        sp.wait_ge(o_free, NCH * (t + 1))
                        sp.dma_start(den[:, :], ot[par][DH:P:32, :]).then_inc(den_moved, 16)
                    elif stage == "spread":
                        sp.wait_ge(recip_done, t + 1)
                        sp.dma_start(recip_rows[DH:P:32, :], den[:, :]).then_inc(recip_moved, 16)
                    elif (stage, i) == ("stack", 0):
                        attended, split = UNITS * (t - 1), NCH * (t + 1)
                        at_least(sp, scores_ready, attended)
                        sp.wait_ge(part1_done, split)
                        sp.wait_ge(part2_done, split)
                        sp.wait_ge(part3_done, split)
                        stack_parts(par, range(3))
                    elif stage == "stack":
                        stack_parts(par, range(3, 6))
                    elif stage == "shift":
                        sp.wait_ge(shift_step, 3 * (t + 1))
                        for n in range(3):
                            row = slice(ROWS + n, ROWS + n + 1)
                            sp.dma_start(qs[par][row, :, :], m_part[:, n, :]).then_inc(shifted, 16)
                    elif stage == "load":
                        sp.wait_ge(side_free, g)
                        load_x(pair)
                    elif stage == "tokenise" and isinstance(pair, int) and pair == 0 and i == 2:
                        sp.wait_ge(side_full, 3)
                        load_x(1)
                    elif stage == "tokenise" and isinstance(pair, int) and pair == 0 and i == 3:
                        freed(sp, 2, g)
                        sp.dma_start(h_res[:, :], h_new[:, :]).then_inc(h_copied, 16)
                    elif stage == "finish" and i == 5 and par == 1:
                        freed(sp, 5, g)
                        sp.dma_start(h2_all[:, bass.ds(pair, 1), :].rearrange("p o l -> p (o l)"), h_res[:, :])\
                          .then_inc(h_stored, 16)
                        if not (isinstance(t, int) and t == B - 1):
                            sp.wait_ge(h_stored, 16 * (pair + 1))
                            sp.dma_start(h_res[:, :], h_new[:, :]).then_inc(h_copied, 16)

                run_phase1(nc.sync, attend_unit, side, lambda b, par: None,
                           lambda eng, name, i, p: store_gates(sp, p) if name == "turn" else None)
                sp.wait_ge(ffn_loaded, 16 * N_FFN)

            @block.gpsimd
            def _(pool):
                def side(stage, i, t, par, pair, g):
                    if stage == "project":
                        pool.wait_ge(part2_done, NCH * t + i + 1)
                        at_least(pool, stacked, 16 * 12 * t)
                        nc.gpsimd.tensor_tensor(qk_part[2][:, chunk[i]], qk_rest[:, chunk[i]], qk_part[1][:, chunk[i]],
                                                ALU.subtract).then_inc(part3_done, 1)
                    elif stage == "finish" and i % 2 == 0:
                        freed(pool, i, g)
                        c = i // 2
                        nc.gpsimd.tensor_tensor(on[:, chunk[c]], ot[par][:, chunk[c]], recip[:, chunk[c]], ALU.mult)\
                          .then_inc(on_ready, 1)

                run_phase1(nc.gpsimd, lambda b, par, u, g: None, side, lambda b, par: None)

            @block.scalar
            def _(act):
                act.wait_ge(setup_psum, 1)
                nc.scalar.activation(qkT[:, :], banks[0][:, 0:P], ACT.Copy)
                act.wait_ge(preset, 2)
                for i in range(2):
                    rows = slice(D * i, D * i + D)
                    nc.scalar.activation(vT[rows, i, :], banks[0][rows, P:P + D], ACT.Copy)
                nc.scalar.activation(biases[:, :], banks[0][:, 2 * P:2 * P + E + E // 2], ACT.Copy)
                nc.scalar.activation(projT[:, :], banks[0][:, P + D:P + 2 * D], ACT.Copy).then_inc(setup_done, 1)

                def evacuate_o(b, par, qc):
                    act.wait_ge(o_ready, NCH * b + qc + 1)
                    nc.scalar.activation(ot[par][:, chunk[qc]], o_bank[:, 0:CH], ACT.Copy).then_inc(o_free, 1)

                def attend_unit(b, par, u, g):
                    qc, r = divmod(u, 1 + KT * H)
                    act.wait_ge(scores_ready, UNITS * b + u + 1)
                    src = score_bank[u % 3][:, 0:CH]
                    if r == 0:
                        nc.scalar.activation(probs_tail[qc][:, :], src, ACT.Exp, scale=SCALE).then_inc(exp_done, 1)
                        return
                    kt, h = divmod(r - 1, H)
                    group = KT * qc + kt
                    if h == 0:
                        at_least(act, pv_done, GROUPS * b + group - 2)
                    nc.scalar.activation(probs[:, group % 3, h, :], src, ACT.Exp, scale=SCALE).then_inc(exp_done, 1)
                    if r == 6 and qc > 0:
                        evacuate_o(b, par, qc - 1)

                def side(stage, i, t, par, pair, g):
                    if stage == "project":
                        bank = full(act, i, g)
                        at_least(act, stacked, 16 * 12 * t)
                        nc.scalar.activation(qk_part[0][:, chunk[i]], bank[:, 0:CH], ACT.Copy).then_inc(part1_done, 1)
                    elif stage == "values":
                        bank = full(act, i, g)
                        if i == 0:
                            nc.scalar.activation(v_tiles[par][:, :, :, 0:DH].rearrange("p k h d -> p (k h) d"),
                                                 bank[:, :].rearrange("p (k d) -> p k d", d=DH), ACT.Copy)\
                              .then_inc(side_free, 1)
                        else:
                            for h in range(H):
                                rows = slice(32 * h, 32 * h + 32)
                                last = nc.scalar.activation(v_tail[par][rows, 32 * h:32 * h + DH], bank[rows, 0:DH], ACT.Copy)
                            last.then_inc(side_free, 1)
                    elif stage == "tokenise" and i in (0, 2):
                        bank = full(act, i, g)
                        at_least(act, h_copied, 16 * pair)
                        cols, n = (slice(0, HALF), HALF) if i == 0 else (slice(IMG, L), TXT)
                        nc.scalar.activation(h_new[:, cols], bank[:, 0:n], ACT.Copy).then_inc(side_free, 1)
                    elif stage == "tokenise" and 3 <= i < 6:
                        c = i - 3
                        bank = full(act, i, g)
                        nc.scalar.activation(xc[:, chunk[c]], bank[:, 0:CH], ACT.Copy)
                        nc.scalar.activation(sq[:, chunk[c]], bank[:, 0:CH], ACT.Square).then_inc(side_free, 1)
                    elif stage == "finish" and i % 2 == 0:
                        bank = full(act, i, g)
                        nc.scalar.activation(recip[:, chunk[i // 2]], bank[:, 0:CH], ACT.Copy).then_inc(side_free, 1)

                run_phase1(nc.scalar, attend_unit, side, lambda b, par: evacuate_o(b, par, NCH - 1), norm_scalar)

            @block.vector
            def _(dve):
                nc.vector.memset(proj_in[:, :, :], 0.0).then_inc(preset, 1)
                nc.vector.memset(vT[:, :, :], 0.0).then_inc(preset, 1)
                nc.vector.memset(root_work[:, :, :], 1.0).then_inc(preset, 1)
                for i in range(2):
                    nc.vector.memset(v_tiles[i][:, :, :, :], 0.0).then_inc(preset, 1)
                    nc.vector.memset(v_tail[i][:, :], 0.0).then_inc(preset, 1)
                    nc.vector.memset(ks[i][ROWS:ROWS + 3, :, :], 1.0).then_inc(preset, 1)
                nc.vector.memset(negm[:, :, :], 0.0).then_inc(preset, 1)
                nc.vector.memset(recip_rows[:, :], 0.0).then_inc(preset, 1)
                dve.wait_ge(preset, 11)
                for i in range(2):
                    nc.vector.memset(v_tiles[i][:, :, :, DH:DH + 1], 1.0).then_inc(preset, 1)
                    for h in range(H):
                        nc.vector.memset(v_tail[i][32 * h:32 * h + 32, 32 * h + DH:32 * h + DH + 1], 1.0)\
                          .then_inc(preset, 1)
                dve.wait_ge(setup_psum, 2)
                nc.vector.tensor_copy(tok_m[:, :, :].rearrange("p k d -> p d k"),
                                      banks[1][:, :].rearrange("p (d k) -> p d k", k=8)).then_inc(setup_done, 1)

                def side(stage, i, t, par, pair, g):
                    if stage == "recip":
                        dve.wait_ge(den_moved, 16 * (t + 1))
                        nc.vector.reciprocal(den[:, :], den[:, :]).then_inc(recip_done, 1)
                    elif stage == "maxima":
                        n = MAXU * t + i
                        dve.wait_ge(max_scores, n + 1)
                        src = max_bank[i % 3]
                        if i < 2 * QT:
                            nc.vector.tensor_reduce(max_parts[:, i // 2, i % 2:i % 2 + 1], src[:, :], AX.X, ALU.max)\
                              .then_inc(max_done, 1)
                        elif i < 2 * QT + 2:
                            part = slice(16 * (i - 2 * QT), 16 * (i - 2 * QT) + 16)
                            nc.vector.tensor_reduce(max_parts[:, part, 2],
                                                    src[:, :].rearrange("p (n k) -> p n k", k=TXT), AX.X, ALU.max)\
                              .then_inc(max_done, 1)
                        else:
                            c = i - 2 * QT - 2
                            nc.vector.tensor_reduce(max_tail[:, c:c + 1], src[:, 0:CH], AX.X, ALU.max)\
                              .then_inc(max_done, 1)
                        if i == MAXU - 1:
                            dve.wait_ge(max_done, MAXU * (t + 1))
                            nc.vector.tensor_reduce(
                                negm[:, 0, 0:H * QTP].rearrange("p (h k) -> p h k", h=H)[:, :, 0:KT],
                                max_parts[:, :, :].rearrange("p (h k) n -> p h k n", h=H), AX.X, ALU.max, negate=True)
                            for h in range(H):
                                rows, col = slice(32 * h, 32 * h + 32), QTP * h + KT
                                last = nc.vector.tensor_reduce(negm[rows, 1, col:col + 1], max_tail[rows, :],
                                                               AX.X, ALU.max, negate=True)
                            last.then_inc(neg_max, 1)
                    elif stage == "shift":
                        bank = full(dve, 0, g)
                        at_least(dve, shifted, 16 * SHIFT_DMAS * t)
                        src = bank[0:H * QTP, 0:P]
                        nc.vector.tensor_copy(m_part[:, 0, :], src).then_inc(shift_step, 1)
                        dve.wait_ge(shift_step, 3 * t + 1)
                        nc.vector.tensor_tensor(m_rest[:, :], src, m_part[:, 0, :], ALU.subtract)\
                          .then_inc(side_free, 1)
                        freed(dve, 0, g)
                        nc.vector.tensor_copy(m_part[:, 1, :], m_rest[:, :]).then_inc(shift_step, 1)
                        dve.wait_ge(shift_step, 3 * t + 2)
                        nc.vector.tensor_tensor(m_part[:, 2, :], m_rest[:, :], m_part[:, 1, :], ALU.subtract)\
                          .then_inc(shift_step, 1)
                    elif stage == "project":
                        dve.wait_ge(part1_done, NCH * t + i + 1)
                        at_least(dve, part3_done, NCH * t)
                        at_least(dve, stacked, 16 * 12 * t)
                        nc.vector.tensor_tensor(qk_rest[:, chunk[i]], step_bank(i, g)[:, 0:CH], qk_part[0][:, chunk[i]],
                                                ALU.subtract).then_inc(side_free, 1)
                        freed(dve, i, g)
                        nc.vector.tensor_copy(qk_part[1][:, chunk[i]], qk_rest[:, chunk[i]]).then_inc(part2_done, 1)
                    elif stage == "tokenise" and i == 1:
                        bank = full(dve, i, g)
                        at_least(dve, h_copied, 16 * pair)
                        nc.vector.tensor_copy(h_new[:, HALF:IMG], bank[:, :]).then_inc(side_free, 1)
                    elif stage == "tokenise" and i == 6:
                        inverse_roots(dve, roots[:, :], root_work, full(dve, i, g), roots_step, pair).then_inc(side_free, 1)
                    elif stage == "tokenise" and i > 6:
                        bank, tokens = full(dve, i, g), wide[i - 7]
                        nc.vector.tensor_tensor(xn[:, tokens], xc[:, tokens], bank[:, 0:tokens.stop - tokens.start],
                                                ALU.mult).then_inc(side_free, 1)
                    elif stage == "finish":
                        c = i // 2
                        if i % 2 == 1:
                            bank = full(dve, i, g)
                            rows = slice(D * par, D * par + D)
                            dve.wait_ge(h_copied, 16 * (pair + 1))
                            dve.wait_ge(ffn_loaded, 16 * N_FFN)
                            nc.vector.scalar_tensor_tensor(out=h_res[rows, chunk[c]], in0=bank[rows, 0:CH],
                                                           scalar=proj_bias[rows, :], in1=h_res[rows, chunk[c]],
                                                           op0=ALU.add, op1=ALU.add).then_inc(side_free, 1)

                def attend_unit(b, par, u, g):
                    if not (isinstance(b, int) and b == B - 1 and u == UNITS // 2):
                        return
                    rest = qk_rest[:, 0:E * HID].rearrange("p (e n) -> p e n", e=E)
                    low, high = slice(0, D), slice(D, P)
                    v = nc.vector
                    v.tensor_copy(w01[:, :, :], w1_sb[:, :, :]).then_inc(w_split, 1)
                    dve.wait_ge(w_split, 1)
                    v.tensor_tensor(rest, w1_sb[:, :, :], w01[:, :, :], ALU.subtract).then_inc(w_split, 1)
                    dve.wait_ge(w_split, 2)
                    v.tensor_copy(w10[:, :, :], rest).then_inc(w_split, 1)
                    dve.wait_ge(w_split, 3)
                    v.tensor_tensor(w20[low, :, :], rest[low], w10[low, :, :], ALU.subtract).then_inc(w_split, 1)
                    v.tensor_copy(w20[high, :, :], w01[high, :, :]).then_inc(w_split, 1)
                    dve.wait_ge(w_split, 5)
                    v.tensor_copy(w01[high, :, :], w10[high, :, :]).then_inc(w_split, 1)
                    dve.wait_ge(w_split, 6)
                    v.tensor_copy(w10[high, :, :], w20[high, :, :]).then_inc(w_split, 1)

                run_phase1(nc.vector, attend_unit, side, lambda b, par: None, norm_vector)

            @block.tensor
            def _(pe):
                pe.wait_ge(setup_loaded, 16 * N_SETUP)
                nc.tensor.transpose(banks[0][:, 0:P], qkv_in[:, :, :].rearrange("p a c -> p (a c)"), ident)
                nc.tensor.transpose(banks[0][:, P:P + D], v_in[:, :, :].rearrange("p a c -> p (a c)"), ident[0:D, 0:D])
                nc.tensor.transpose(banks[0][:, P + D:P + 2 * D], proj_in[:, :, :].rearrange("p h d -> p (h d)"),
                                    ident[0:D, 0:D])
                nc.tensor.transpose(banks[0][:, 2 * P:2 * P + E + E // 2], bias_in[:, :],
                                    ident[0:E + E // 2, 0:E + E // 2]).then_inc(setup_psum, 1)
                for d in range(D):
                    for th in range(2):
                        last = nc.tensor.matmul(banks[1][C * th:C * th + C, 8 * d:8 * d + 8], tok_in[:, d, :],
                                                cst[0:2 * NFREQ, C_DFT + 8 * th:C_DFT + 8 * th + 8],
                                                start=True, stop=True)
                last.then_inc(setup_psum, 1)
                pe.wait_ge(setup_done, 2)
                pe.wait_ge(preset, PRESETS)

                def heads_times_v(b, par, group, g):
                    qc, kt = divmod(group, KT)
                    pe.wait_ge(exp_done, UNITS * b + (1 + KT * H) * qc + 1 + H * kt + H)
                    if kt == 0:
                        at_least(pe, o_free, NCH * b + qc)
                        if qc == 0:
                            pe.wait_ge(side_free, g)
                    for h in range(H):
                        last = nc.tensor.matmul(o_bank[32 * h:32 * h + 32, 0:CH], v_tiles[par][:, kt, h, :],
                                                probs[:, group % 3, h, :], start=(kt == 0), stop=False,
                                                skip_group_check=True)
                    last.then_inc(pv_done, 1)
                    if kt == KT - 1:
                        nc.tensor.matmul(o_bank[:, 0:CH], v_tail[par][:, :], probs_tail[qc][:, :], start=False, stop=True,
                                         skip_group_check=True).then_inc(o_ready, 1)

                def attend_unit(b, par, u, g):
                    qc, r = divmod(u, 1 + KT * H)
                    if u == 0:
                        pe.wait_ge(shifted, 16 * SHIFT_DMAS * (b + 1))
                    at_least(pe, exp_done, UNITS * b + u - 2)
                    bank = score_bank[u % 3]
                    if r == 0:
                        for h in range(H):
                            last = nc.tensor.matmul(bank[32 * h:32 * h + 32, 0:CH], ks[par][0:ROWS + 3, h, IMG:L],
                                                    qs[par][0:ROWS + 3, h, chunk[qc]], start=True, stop=True)
                    else:
                        kt, h = divmod(r - 1, H)
                        last = nc.tensor.matmul(bank[:, 0:CH], ks[par][0:ROWS + 3, h, P * kt:P * kt + P],
                                                qs[par][0:ROWS + 3, h, chunk[qc]], start=True, stop=True)
                    last.then_inc(scores_ready, 1)
                    chunk_of, step = divmod(u - PV_LAG, 1 + KT * H)
                    if chunk_of >= 0 and step % H == 0 and step < H * KT:
                        heads_times_v(b, par, KT * chunk_of + step // H, g)

                def embed(bank, half, part):
                    next_block, t4 = divmod(part, 4)
                    first = NPATCH // 2 * half + next_block
                    for bp in range(2):
                        last = nc.tensor.matmul(bank[D * bp:D * bp + D, :], tok_m[:, part, :],
                                                xt[bp][:, first:first + NPATCH // 2, t4, :],
                                                start=(part == 0), stop=(part == 7), skip_group_check=True)
                    return last

                def side(stage, i, t, par, pair, g):
                    rows = None if par is None else slice(D * par, D * par + D)
                    if stage == "maxima":
                        n = MAXU * t + i
                        if i == 0:
                            pe.wait_ge(stacked, 16 * 12 * (t + 1))
                        at_least(pe, max_done, n - 2)
                        bank = max_bank[i % 3]
                        if i < 2 * QT:
                            h, qt = divmod(i // 2, KT)
                            last = nc.tensor.matmul(bank[:, :], qs[par][0:ROWS, h, P * qt:P * qt + P],
                                                    ks[par][0:ROWS, h, HALF * (i % 2):HALF * (i % 2) + HALF],
                                                    start=True, stop=True)
                        elif i < 2 * QT + 2:
                            for j in range(16):
                                h, qt = divmod(16 * (i - 2 * QT) + j, KT)
                                last = nc.tensor.matmul(bank[:, TXT * j:TXT * j + TXT], qs[par][0:ROWS, h, P * qt:P * qt + P],
                                                        ks[par][0:ROWS, h, IMG:L], start=True, stop=True)
                        else:
                            c = i - 2 * QT - 2
                            for h in range(H):
                                last = nc.tensor.matmul(bank[32 * h:32 * h + 32, 0:CH], qs[par][0:ROWS, h, IMG:L],
                                                        ks[par][0:ROWS, h, chunk[c]], start=True, stop=True)
                        last.then_inc(max_scores, 1)
                        return
                    if stage == "embed":
                        half, part = i
                        if part == 0:
                            if half == 0:
                                pe.wait_ge(x_loaded, 16 * X_DMAS * (pair + 1))
                            if not all_free(half, g):
                                freed(pe, half - 1, g)
                        embed(step_bank(half, g), half, part)
                        return
                    if stage in ("spread", "stack", "load", "recip"):
                        return
                    bank = step_bank(i, g)
                    if not all_free(i, g):
                        freed(pe, i - 1, g)
                    if stage == "shift":
                        pe.wait_ge(neg_max, t + 1)
                        nc.tensor.matmul(bank[:, 0:P], negm[:, 0, :], ident, start=True, stop=False,
                                         skip_group_check=True)
                        last = nc.tensor.matmul(bank[:, 0:TXT], negm[:, 1, :], cst[:, C_TAIL:C_TAIL + TXT],
                                                start=False, stop=True, skip_group_check=True)
                    elif stage == "project":
                        last = nc.tensor.matmul(bank[:, 0:CH], qkT[rows, :], xn[rows, chunk[i]], start=True, stop=True)
                    elif stage == "values":
                        if i == 0:
                            for tile in range(KT):
                                last = nc.tensor.matmul(bank[:, D * tile:D * tile + D], xn[:, P * tile:P * tile + P],
                                                        vT[:, par, :], start=True, stop=True)
                        else:
                            for h in range(H):
                                last = nc.tensor.matmul(bank[32 * h:32 * h + 32, 0:DH], xn[:, IMG:L],
                                                        vT[:, par, DH * h:DH * h + DH], start=True, stop=True)
                    elif stage == "tokenise":
                        if i < 2:
                            last = embed(bank, i, 7)
                        elif i == 2:
                            last = nc.tensor.matmul(bank[:, 0:TXT], text_in[:, :, :].rearrange("t b d -> t (b d)"),
                                                    ident[0:TXT, 0:TXT], start=True, stop=True)
                        elif i < 6:
                            last = nc.tensor.matmul(bank[:, 0:CH], centre, h_new[:, chunk[i - 3]], start=True, stop=True)
                        elif i == 6:
                            last = token_variances(bank, sq)
                        else:
                            last = spread_roots(bank, roots, i - 7)
                    elif stage == "finish":
                        c = i // 2
                        if i == 0:
                            pe.wait_ge(recip_moved, 16 * (t + 1))
                        if i % 2 == 0:
                            last = nc.tensor.matmul(bank[:, 0:CH], den_sel, recip_rows[:, chunk[c]], start=True, stop=True)
                        else:
                            pe.wait_ge(on_ready, NCH * t + c + 1)
                            last = nc.tensor.matmul(bank[rows, 0:CH], projT[:, :], on[:, chunk[c]], start=True, stop=True)
                    last.then_inc(side_full, 1)

                run_phase1(nc.tensor, attend_unit, side, lambda b, par: heads_times_v(b, par, GROUPS - 1, None),
                           norm_tensor)

        phase1.close()

        x01 = sb("x01", [P, B, L], BF16)
        x02 = sb("x02", [P, B, L], BF16)
        cwb = [sb(f"cwb{i}", [P, E // 2, L]) for i in range(2)]
        h2 = [sb(f"h2_{i}", [D, L]) for i in range(2)]
        hid = sb("hid", [P, 4, CH])
        prod = sb("prod", [P, 4, CH])
        acc = sb("acc", [P, 2, L])
        outs = [sb(f"outs{i}", [P, KT, D]) for i in range(2)]
        out_tail = [sb(f"out_tail{i}", [TXT, D]) for i in range(2)]

        AT_NORM = {0: [("centre", 0)], 1: [("centre", 1)], 2: [("centre", 2)],
                   3: [("roots", 0)], 5: [("scale", 0)], 6: [("scale", 1)], 7: [("scale", 2)], 9: [("gates", 0)],
                   10: [("split", 0), ("choose", 0)], 11: [("split", 1), ("choose", 1)],
                   12: [("split", 2), ("choose", 2)], 13: [("choose", 3)], 14: [("choose", 4)], 15: [("choose", 5)],
                   16: [("turn", 0)]}
        FOLD_LAST, FOLD_FIRST = 8, 20

        def run_phase2(eng, product, norm_step, fold_batch, step_first=False):
            def pair(n):
                ends = isinstance(n, int) and n == PAIRS - 1
                for m in range(2 * YPB):
                    bp, place = divmod(m, YPB)
                    c, k = divmod(place, 4)
                    if not step_first:
                        product(2 * n + bp, bp, c, k, n)
                    for name, i in [] if ends else AT_NORM.get(m, []):
                        norm_step(eng, name, i, n + 1)
                    if step_first:
                        product(2 * n + bp, bp, c, k, n)
                    if m == FOLD_LAST and not (isinstance(n, int) and n == 0):
                        fold_batch(2 * n - 1, 1, NORM_FILLS * (n + 1) + (0 if ends else GATES))
                    if m == FOLD_FIRST:
                        fold_batch(2 * n, 0, NORM_FILLS * (n + 1) + (0 if ends else NORM_FILLS))

            pair(0)
            with eng.Fori(1, PAIRS - 1) as n:
                pair(n)
            pair(PAIRS - 1)

        with nc.Block() as block:
            @block.sync
            def _(sp):
                def stack(b):
                    sp.wait_ge(x_split, 3 * (b // 2) + 3)
                    rows = slice(D * (b % 2), D * (b % 2) + D)
                    for half, to, part in ((0, x01, 0), (1, x01, 1), (0, x02, 0), (1, x02, 2)):
                        sp.dma_start(to[D * half:D * half + D, b, :], x_part[part][rows, :])\
                          .then_inc(x_stacked[b % 2], 16)

                def load_gates(b):
                    at_least(sp, y_read, YPB * (b - 1))
                    for o in range(2):
                        src = cw_dram.rearrange("(k o) (b l) -> o b k l", o=2, b=B)[o, b]
                        sp.dma_start(cwb[b % 2][D * o:D * o + D, :, :],
                                     src.unsqueeze(0).broadcast_to([D, E // 2, L])).then_inc(cw_loaded[b % 2], 16)

                def load_h2(b):
                    rows = slice(D * (b % 2), D * (b % 2) + D)
                    sp.dma_start(h2[b % 2][:, :], h2_all[rows, b // 2, :]).then_inc(h2_loaded[b % 2], 16)

                def store(b):
                    sp.wait_ge(out_read, b + 1)
                    rows = out[b, 0:IMG, :].rearrange("(v t o) c -> o v t c", t=KT, o=2)
                    for o in range(2):
                        sp.dma_start(rows[o], outs[b % 2][V * o:V * o + V, :, :]).then_inc(out_stored, 16)
                    sp.dma_start(out[b, IMG:L, :], out_tail[b % 2][:, :]).then_inc(out_stored, 16)
                    sp.wait_ge(out_stored, 16 * 3 * (b + 1))
                    if b + 2 < B:
                        load_h2(b + 2)

                stack(0)
                load_gates(0)
                stack(1)
                for b in range(2):
                    load_h2(b)
                for n in range(PAIRS):
                    load_gates(2 * n + 1)
                    if n > 0:
                        store(2 * n - 1)
                    if n + 1 < PAIRS:
                        stack(2 * n + 2)
                        stack(2 * n + 3)
                        store_gates(sp, n + 1)
                        load_gates(2 * n + 2)
                    store(2 * n)
                store(B - 1)

            @block.gpsimd
            def _(pool):
                def product(b, bp, c, k, n):
                    if k == 0:
                        return
                    dst = acc[:, bp, chunk[c]]
                    first = YPB * b + 4 * c
                    if (c, k) == (0, 1):
                        at_least(pool, out_full, b - 1)
                    at_least(pool, summed, first + k - 1)
                    pool.wait_ge(y_read, first + k + 1)
                    nc.gpsimd.tensor_tensor(dst, prod[:, 0, :] if k == 1 else dst, prod[:, k, :], ALU.add)\
                      .then_inc(summed, 1)
                    if k == 3:
                        if c == 0:
                            pool.wait_ge(h2_loaded[bp], 16 * (n + 1))
                        pool.wait_ge(summed, first + 3)
                        nc.gpsimd.tensor_tensor(acc[0:D, bp, chunk[c]], acc[0:D, bp, chunk[c]], h2[bp][:, chunk[c]],
                                                ALU.add).then_inc(summed, 1)

                run_phase2(nc.gpsimd, product, lambda eng, name, i, p: None, lambda b, bp, fills: None, step_first=True)

            @block.scalar
            def _(act):
                def product(b, bp, c, k, n):
                    for e in (2 * k, 2 * k + 1):
                        act.wait_ge(hid_full, KPB * b + E * c + e + 1)
                        at_least(act, y_full, YPB * b + (E * c + e) // 2 - 1)
                        nc.scalar.activation(hid[:, e % 4, :], banks[e % 4][:, 0:CH], ACT.Gelu,
                                             bias=b1_sb[:, e:e + 1]).then_inc(gelu_done, 1)

                def evacuate_out(b, bp, fills):
                    act.wait_ge(out_full, b + 1)
                    nc.scalar.activation(outs[bp][:, :, :].rearrange("p t c -> p (t c)"), banks[6][:, :], ACT.Copy)
                    nc.scalar.activation(out_tail[bp][:, :], banks[7][0:TXT, 0:D], ACT.Copy).then_inc(out_read, 1)

                run_phase2(nc.scalar, product, norm_scalar, evacuate_out)
                evacuate_out(B - 1, 1, 0)

            @block.vector
            def _(dve):
                def product(b, bp, c, k, n):
                    if (c, k) == (0, 0):
                        dve.wait_ge(cw_loaded[bp], 16 * 2 * (n + 1))
                    dve.wait_ge(y_full, YPB * b + 4 * c + k + 1)
                    at_least(dve, summed, YPB * b + 4 * (c - 1) + max(k, 1))
                    nc.vector.scalar_tensor_tensor(out=prod[:, k, :], in0=banks[4 + k % 2][:, 0:CH], scalar=b2_sb[:, k:k + 1],
                                           in1=cwb[bp][:, k, chunk[c]], op0=ALU.add, op1=ALU.mult).then_inc(y_read, 1)

                run_phase2(nc.vector, product, norm_vector, lambda b, bp, fills: None, step_first=True)

            @block.tensor
            def _(pe):
                def experts_out(b, bp, c, k):
                    pe.wait_ge(gelu_done, KPB * b + E * c + 2 * k + 2)
                    at_least(pe, y_read, YPB * b + 4 * c + k - 1)
                    for o in range(2):
                        e = 2 * k + o
                        last = nc.tensor.matmul(banks[4 + k % 2][D * o:D * o + D, 0:CH], w2_sb[:, e, :],
                                                hid[:, e % 4, :], start=True, stop=True)
                    last.then_inc(y_full, 1)

                def product(b, bp, c, k, n):
                    if (c, k) == (0, 0):
                        pe.wait_ge(x_stacked[bp], 16 * X_STACKS * (n + 1))
                        if isinstance(b, int) and b == 0:
                            pe.wait_ge(w_split, 7)
                    for e in (2 * k, 2 * k + 1):
                        at_least(pe, gelu_done, KPB * b + E * c + e - 3)
                        for i, (w, xs) in enumerate(((w01, x01), (w10, x01), (w20, x02))):
                            last = nc.tensor.matmul(banks[e % 4][:, 0:CH], w[:, e, :],
                                                    xs[:, bass.ds(b, 1), chunk[c]].rearrange("p o l -> p (o l)"),
                                                    start=(i == 0), stop=(i == 2))
                        last.then_inc(hid_full, 1)
                    if k > 0:
                        experts_out(b, bp, c, k - 1)
                    elif c > 0:
                        experts_out(b, bp, c - 1, 3)
                    elif bp > 0 or not (isinstance(n, int) and n == 0):
                        experts_out(b - 1, 1 - bp, NCH - 1, 3)

                def fold_batch(b, bp, fills):
                    pe.wait_ge(norm_read, fills)
                    at_least(pe, out_read, b)
                    pe.wait_ge(summed, YPB * (b + 1))
                    for t in range(KT):
                        nc.tensor.matmul(banks[6][:, D * t:D * t + D], acc[:, bp, P * t:P * t + P], fold,
                                         start=True, stop=True)
                    nc.tensor.matmul(banks[7][0:TXT, 0:D], acc[:, bp, IMG:L], fold, start=True, stop=True)\
                      .then_inc(out_full, 1)

                run_phase2(nc.tensor, product, norm_tensor, fold_batch)
                experts_out(B - 1, 1, NCH - 1, 3)
                fold_batch(B - 1, 1, NORM_FILLS * PAIRS)


def constants():
    import numpy as np

    c = np.zeros((P, C_COLS), np.float32)
    i = np.arange(P)
    same = (i[:, None] // D == i[None, :] // D) / D
    c[:, C_ID:C_ID + P] = np.eye(P)
    c[:, C_CENTRE:C_CENTRE + P] = np.eye(P) - same
    c[:, C_MEAN:C_MEAN + P] = same
    c[:, C_TAIL:C_TAIL + TXT] = i[:, None] % 32 == np.arange(TXT)[None, :]
    c[:, C_DEN:C_DEN + P] = (i[:, None] // 32 == i[None, :] // 32) & (i[:, None] % 32 == DH)
    c[:, C_FOLD:C_FOLD + D] = i[:, None] % D == np.arange(D)[None, :]
    t = np.arange(PATCH).reshape(2, 2, 4).transpose(1, 0, 2).reshape(PATCH)
    angle = 2 * np.pi * np.arange(NFREQ)[:, None] * t[None, :] / PATCH
    c[0:NFREQ, C_DFT:C_DFT + PATCH] = np.cos(angle) / np.sqrt(PATCH)
    c[NFREQ:2 * NFREQ, C_DFT:C_DFT + PATCH] = -np.sin(angle) / np.sqrt(PATCH)
    c[:, C_ORDER:C_ORDER + E] = E - np.arange(E)
    return c


_INS = ["x", "txt", "L0_tok_W", "L0_attn_w_qkv", "L0_attn_w_proj", "L0_attn_b_proj", "L0_ffn_gate_w",
        "L0_ffn_gate_b", "L0_ffn_W1", "L0_ffn_b1", "L0_ffn_W2", "L0_ffn_b2"]


def kernel(**inputs):
    import numpy as np
    import concourse.bacc as bacc
    from concourse.bass_utils import run_bass_kernel_spmd

    nc = bacc.Bacc("TRN2", target_bir_lowering=False, num_devices=1)
    arrays = {f"in_{name}": np.ascontiguousarray(inputs[name]) for name in _INS}
    arrays["in_constants"] = constants()
    args = [nc.dram_tensor(n, a.shape, mybir.dt.from_np(a.dtype), kind="ExternalInput").ap() for n, a in arrays.items()]
    out = nc.dram_tensor("out_0", (B, L, D), F32, kind="ExternalOutput").ap()
    build(nc, *args, out)
    return run_bass_kernel_spmd(nc, [arrays], core_ids=[0]).results[0]["out_0"]
```
